# Optimizing a Trainium2 kernel written in Bass

```python
import numpy as np
import jax
import jax.numpy as jnp

def _softmax(x, axis=-1):
    return jax.nn.softmax(x, axis=axis)

def _gelu(x):
    return jax.nn.gelu(x, approximate=True)

def _silu(x):
    return jax.nn.silu(x)

def _sigmoid(x):
    return jax.nn.sigmoid(x)

def _layernorm(x, axis=-1, eps=1e-05):
    m = jnp.mean(x, axis=axis, keepdims=True)
    v = jnp.var(x, axis=axis, keepdims=True)
    return (x - m) / jnp.sqrt(v + eps)

def _scatter_add(tgt, idx, src, axis=0):
    return tgt.at[idx].add(src)

def _segment_sum(src, seg, n):
    return jax.ops.segment_sum(src, seg, n)
kernel_name = 'mk_seq_preln_d1_jaxref_r4_1a1d56'

def setup_inputs(seed: int=0):
    np.random.seed(seed)
    _w = jnp.asarray

    def _L0_attn_setup():
        import jax, jax.numpy as jnp
        import numpy as np
        D_MODEL = 512
        D_INNER = 1024
        D_STATE = 16
        DT_RANK = 128
        D_CONV = 4
        EPS = 1e-05

        def _rmsnorm(x, w):
            return x * jax.lax.rsqrt(jnp.mean(jnp.square(x), axis=-1, keepdims=True) + EPS) * w

        def _depthwise_causal_conv(x, conv_w, conv_b):
            k = conv_w[:, None, :]
            y = jax.lax.conv_general_dilated(x, k, window_strides=(1,), padding=((D_CONV - 1, 0),), dimension_numbers=('NWC', 'WIO', 'NWC'), feature_group_count=D_INNER)
            return y + conv_b

        def _selective_scan(u, delta, A, B, C, D):
            deltaA = jnp.exp(jnp.einsum('bld,dn->bldn', delta, A))
            deltaBu = jnp.einsum('bld,bln,bld->bldn', delta, B, u)
            dA = jnp.moveaxis(deltaA, 1, 0)
            dBu = jnp.moveaxis(deltaBu, 1, 0)
            Ct = jnp.moveaxis(C, 1, 0)
            b, l, d = u.shape
            n = A.shape[1]

            def step(h, inputs):
                dA_t, dBu_t, C_t = inputs
                h = h * dA_t + dBu_t
                y = jnp.einsum('bdn,bn->bd', h, C_t)
                return (h, y)
            h0 = jnp.zeros((b, d, n), u.dtype)
            _, ys = jax.lax.scan(step, h0, (dA, dBu, Ct))
            y = jnp.moveaxis(ys, 0, 1)
            return y + u * D
        key = jax.random.key(seed)
        ks = jax.random.split(key, 10)
        b, l = (1, 256)
        s = 0.02
        x = jax.random.normal(ks[0], (b, l, D_MODEL), jnp.float32)
        w_norm = jnp.ones((D_MODEL,), jnp.float32)
        W_in = jax.random.normal(ks[1], (D_MODEL, 2 * D_INNER), jnp.float32) * s
        conv_w = jax.random.normal(ks[2], (D_CONV, D_INNER), jnp.float32) * 0.3
        conv_b = jnp.zeros((D_INNER,), jnp.float32)
        W_xp = jax.random.normal(ks[3], (D_INNER, DT_RANK + 2 * D_STATE), jnp.float32) * s
        W_dt = jax.random.normal(ks[4], (DT_RANK, D_INNER), jnp.float32) * s
        b_dt = jnp.full((D_INNER,), -4.0, jnp.float32)
        A_log = jnp.log(jnp.tile(jnp.arange(1, D_STATE + 1, dtype=jnp.float32), (D_INNER, 1)))
        D = jnp.ones((D_INNER,), jnp.float32)
        W_out = jax.random.normal(ks[5], (D_INNER, D_MODEL), jnp.float32) * s
        return dict(x=x, w_norm=w_norm, W_in=W_in, conv_w=conv_w, conv_b=conv_b, W_xp=W_xp, W_dt=W_dt, b_dt=b_dt, A_log=A_log, D=D, W_out=W_out)
    _L0_attn_in = _L0_attn_setup()

    def _L0_ffn_setup():
        import jax, jax.numpy as jnp
        import numpy as np
        from jax import lax
        H = 512
        I = 256
        E = 32
        K = 4
        SH_I = 512
        EPS = 1e-06

        def _rmsnorm(x, w, eps=EPS):
            var = jnp.mean(jnp.square(x.astype(jnp.float32)), axis=-1, keepdims=True)
            return (x * lax.rsqrt(var + eps)).astype(x.dtype) * w
        key = jax.random.key(seed)
        ks = jax.random.split(key, 8)
        s = lambda d: 1.0 / np.sqrt(d)
        return {'x': jax.random.normal(ks[0], (2, 512, H), jnp.float32), 'norm_w': jnp.ones((H,), jnp.float32), 'router_w': jax.random.normal(ks[1], (E, H), jnp.float32) * s(H), 'w1': jax.random.normal(ks[2], (E, H, 2 * I), jnp.float32) * s(H), 'w2': jax.random.normal(ks[3], (E, I, H), jnp.float32) * s(I), 'sg': jax.random.normal(ks[4], (H, SH_I), jnp.float32) * s(H), 'su': jax.random.normal(ks[5], (H, SH_I), jnp.float32) * s(H), 'sd': jax.random.normal(ks[6], (SH_I, H), jnp.float32) * s(SH_I)}
    _L0_ffn_in = _L0_ffn_setup()
    _d = {'L0_attn_x': _L0_attn_in['x'], 'L0_attn_w_norm': _L0_attn_in['w_norm'], 'L0_attn_W_in': _L0_attn_in['W_in'], 'L0_attn_conv_w': _L0_attn_in['conv_w'], 'L0_attn_conv_b': _L0_attn_in['conv_b'], 'L0_attn_W_xp': _L0_attn_in['W_xp'], 'L0_attn_W_dt': _L0_attn_in['W_dt'], 'L0_attn_b_dt': _L0_attn_in['b_dt'], 'L0_attn_A_log': _L0_attn_in['A_log'], 'L0_attn_D': _L0_attn_in['D'], 'L0_attn_W_out': _L0_attn_in['W_out'], 'L0_ffn_norm_w': _L0_ffn_in['norm_w'], 'L0_ffn_router_w': _L0_ffn_in['router_w'], 'L0_ffn_w1': _L0_ffn_in['w1'], 'L0_ffn_w2': _L0_ffn_in['w2'], 'L0_ffn_sg': _L0_ffn_in['sg'], 'L0_ffn_su': _L0_ffn_in['su'], 'L0_ffn_sd': _L0_ffn_in['sd']}
    _x0 = _d['L0_attn_x']
    _d['L0_attn_x'] = jax.random.normal(jax.random.fold_in(jax.random.key(seed), 1), (2, 1024, 512), dtype=_x0.dtype)
    del _x0
    return _d

def reference(L0_attn_x, L0_attn_w_norm, L0_attn_W_in, L0_attn_conv_w, L0_attn_conv_b, L0_attn_W_xp, L0_attn_W_dt, L0_attn_b_dt, L0_attn_A_log, L0_attn_D, L0_attn_W_out, L0_ffn_norm_w, L0_ffn_router_w, L0_ffn_w1, L0_ffn_w2, L0_ffn_sg, L0_ffn_su, L0_ffn_sd):

    def _L0_attn_ref(x, w_norm, W_in, conv_w, conv_b, W_xp, W_dt, b_dt, A_log, D, W_out):
        import jax, jax.numpy as jnp
        import numpy as np
        D_MODEL = 512
        D_INNER = 1024
        D_STATE = 16
        DT_RANK = 128
        D_CONV = 4
        EPS = 1e-05

        def _rmsnorm(x, w):
            return x * jax.lax.rsqrt(jnp.mean(jnp.square(x), axis=-1, keepdims=True) + EPS) * w

        def _depthwise_causal_conv(x, conv_w, conv_b):
            k = conv_w[:, None, :]
            y = jax.lax.conv_general_dilated(x, k, window_strides=(1,), padding=((D_CONV - 1, 0),), dimension_numbers=('NWC', 'WIO', 'NWC'), feature_group_count=D_INNER)
            return y + conv_b

        def _selective_scan(u, delta, A, B, C, D):
            deltaA = jnp.exp(jnp.einsum('bld,dn->bldn', delta, A))
            deltaBu = jnp.einsum('bld,bln,bld->bldn', delta, B, u)
            dA = jnp.moveaxis(deltaA, 1, 0)
            dBu = jnp.moveaxis(deltaBu, 1, 0)
            Ct = jnp.moveaxis(C, 1, 0)
            b, l, d = u.shape
            n = A.shape[1]

            def step(h, inputs):
                dA_t, dBu_t, C_t = inputs
                h = h * dA_t + dBu_t
                y = jnp.einsum('bdn,bn->bd', h, C_t)
                return (h, y)
            h0 = jnp.zeros((b, d, n), u.dtype)
            _, ys = jax.lax.scan(step, h0, (dA, dBu, Ct))
            y = jnp.moveaxis(ys, 0, 1)
            return y + u * D
        xn = _rmsnorm(x, w_norm)
        xz = xn @ W_in
        xs, res = jnp.split(xz, 2, axis=-1)
        xs = _depthwise_causal_conv(xs, conv_w, conv_b)
        xs = jax.nn.silu(xs)
        A = -jnp.exp(A_log)
        xdbc = xs @ W_xp
        dt_r = xdbc[..., :DT_RANK]
        B = xdbc[..., DT_RANK:DT_RANK + D_STATE]
        C = xdbc[..., DT_RANK + D_STATE:]
        delta = jax.nn.softplus(dt_r @ W_dt + b_dt)
        y = _selective_scan(xs, delta, A, B, C, D)
        y = y * jax.nn.silu(res)
        out = y @ W_out + x
        return out

    def _L0_ffn_ref(x, norm_w, router_w, w1, w2, sg, su, sd):
        import jax, jax.numpy as jnp
        import numpy as np
        from jax import lax
        H = 512
        I = 256
        E = 32
        K = 4
        SH_I = 512
        EPS = 1e-06

        def _rmsnorm(x, w, eps=EPS):
            var = jnp.mean(jnp.square(x.astype(jnp.float32)), axis=-1, keepdims=True)
            return (x * lax.rsqrt(var + eps)).astype(x.dtype) * w
        B, S, _ = x.shape
        residual = x
        h = _rmsnorm(x, norm_w)
        flat = h.reshape(-1, H)
        T = flat.shape[0]
        logits = flat.astype(jnp.float32) @ router_w.T
        scores = jax.nn.softmax(logits, axis=-1)
        topk_w, topk_ids = lax.top_k(scores, K)
        topk_w = topk_w / jnp.sum(topk_w, axis=-1, keepdims=True)
        ids = topk_ids.reshape(-1)
        sort_idx = jnp.argsort(ids)
        tok_idx = sort_idx // K
        xs = jnp.take(flat, tok_idx, axis=0)
        group_sizes = jnp.bincount(ids, length=E).astype(jnp.int32)
        gu = lax.ragged_dot(xs, w1, group_sizes)
        g, u = jnp.split(gu, 2, axis=-1)
        act = jax.nn.silu(g) * u
        ys = lax.ragged_dot(act, w2, group_sizes)
        y = jnp.zeros((T * K, H), ys.dtype).at[sort_idx].set(ys)
        routed = jnp.sum(y.reshape(T, K, H) * topk_w[..., None].astype(ys.dtype), axis=1)
        shared = jax.nn.silu(flat @ sg) * (flat @ su) @ sd
        out = residual + (routed + shared).reshape(B, S, H)
        return out
    x = L0_attn_x
    x = x + _L0_attn_ref(_layernorm(x, axis=-1), L0_attn_w_norm, L0_attn_W_in, L0_attn_conv_w, L0_attn_conv_b, L0_attn_W_xp, L0_attn_W_dt, L0_attn_b_dt, L0_attn_A_log, L0_attn_D, L0_attn_W_out)
    x = x + _L0_ffn_ref(_layernorm(x, axis=-1), L0_ffn_norm_w, L0_ffn_router_w, L0_ffn_w1, L0_ffn_w2, L0_ffn_sg, L0_ffn_su, L0_ffn_sd)
    return x

_drawn_inputs = setup_inputs


def setup_inputs(seed=0):
    import zlib

    import numpy as np

    out = dict(_drawn_inputs(seed))
    spreads = {'L0_attn_w_norm': (1.0, 0.2),
     'L0_attn_conv_b': (0.0, 0.1),
     'L0_attn_b_dt': (-4.0, 0.2),
     'L0_attn_D': (1.0, 0.2),
     'L0_ffn_norm_w': (1.0, 0.2)}
    factors = {}
    for name, (base, spread) in spreads.items():
        noise = np.random.default_rng([zlib.crc32(name.encode()), seed]).standard_normal(out[name].shape)
        drawn = base * np.exp(spread * noise) if base else spread * noise
        out[name] = jnp.asarray(drawn.astype(out[name].dtype))
    for name, factor in factors.items():
        out[name] = (out[name] * factor).astype(out[name].dtype)
    return out
```

```python
from contextlib import ExitStack

import numpy as np

import concourse.bass as bass
from concourse import mybir

ALU = mybir.AluOpType
ACT = mybir.ActivationFunctionType
AX = mybir.AxisListType
F32 = mybir.dt.float32
I32 = mybir.dt.int32
U32 = mybir.dt.uint32

P = 128
NB, LEN, DM = 2, 1024, 512
T = NB * LEN
TT = T // P
DI, NS, DR, KW = 1024, 16, 128, 4
KC = DM // P
DC = DI // P
SEG = 512
HALVES = LEN // SEG
ST = SEG // P
Q = 4
NQ = NS // Q
E, FI, TOPK = 32, 256, 4
FC = FI // P
SH = 512
NT = T * TOPK // P + E
RING = 4
EPS_LN, EPS_RMS_A, EPS_RMS_F = 1e-5, 1e-5, 1e-6


class Chain:

    def __init__(self, eng, sem, base=0):
        self.eng, self.sem, self.base, self.n = eng, sem, base, 0

    def add(self, ins):
        ins.then_inc(self.sem, 1)
        self.n += 1

    def settle(self):
        self.eng.wait_ge(self.sem, self.base + self.n)


def bcast(ap, shape):
    return ap.to_broadcast(shape)


def constants(nc, c, ctx, dram):
    sb = lambda name, shape, dt=F32: ctx.enter_context(nc.sbuf_tensor(name, shape, dt))
    c.ident, c.ones, c.tri = sb("ident", [P, P]), sb("ones", [P, P]), sb("tri", [P, P])
    made = ctx.enter_context(nc.semaphore("const_made"))
    with nc.Block() as block:
        @block.gpsimd
        def _(eng):
            eng.memset(c.ident[:], 0.0).then_inc(made, 1)
            eng.memset(c.ones[:], 1.0).then_inc(made, 1)
            eng.wait_ge(made, 2)
            eng.affine_select(out=c.ident[:], in_=c.ident[:], compare_op=ALU.not_equal, fill=1.0, base=0,
                              pattern=[[-1, P]], channel_multiplier=1).then_inc(made, 1)
            eng.affine_select(out=c.tri[:], in_=c.ones[:], compare_op=ALU.is_gt, fill=0.0, base=0,
                              pattern=[[1, P]], channel_multiplier=-1).then_inc(made, 1)
            eng.wait_ge(made, 4)


def mamba(nc, c, dram):
    ctx = ExitStack()
    with ctx:
        def sb(name, shape, dt=F32):
            return ctx.enter_context(nc.sbuf_tensor(name, shape, dt))

        def sem(name):
            return ctx.enter_context(nc.semaphore(name))

        bank = [ctx.enter_context(nc.psum_tensor(f"bank{i}", [P, SEG], F32)) for i in range(8)]
        w_in = sb("w_in", [P, KC, DI])
        w_xp = sb("w_xp", [P, DC, DR + 2 * NS])
        w_out = sb("w_out", [P, DC, DM])
        conv_w, conv_b = sb("conv_w_sb", [P, DC, KW]), sb("conv_b_sb", [P, DC])
        b_dt, d_skip = sb("b_dt_sb", [P, DC]), sb("d_skip", [P, DC])
        a_neg = sb("a_neg", [P, DC * NS])
        norm_w = sb("norm_w_a", [P, DM])
        w_res = sb("w_res", [P, 2, KC, P])
        w_dt = sb("w_dt_sb", [P, 2, P])
        b_rep, c_rep = sb("b_rep", [P, NS, SEG]), sb("c_rep", [P, NS, SEG])
        xin = sb("xin", [P, 2, ST, DM])
        xnT = sb("xnT", [P, KC, SEG])
        xraw = sb("xraw", [P, 2, KW - 1 + SEG])
        hist = sb("hist", [P, DC, KW - 1])
        xs = sb("xs", [P, DC, SEG])
        dtr = sb("dtr", [P, SEG])
        bc = sb("bc", [2 * NS, SEG])
        delta = sb("delta", [P, 2, SEG])
        spl = xraw[:, :, 0:SEG]
        zs = sb("zs", [P, 2, SEG])
        cv = zs
        h = sb("h", [P, NQ, Q, SEG])
        state = sb("state", [P, DC * NS])
        st6, mv = sb("st6", [P, ST, 6]), sb("mv", [P, ST, 2])
        var1, rstd = sb("var1", [P, ST]), sb("rstd", [P, ST])
        ssq, ms, rrms = sb("ssq", [P, ST]), sb("ms", [P, ST]), sb("rrms", [P, ST])
        xl = h[:, 0, :, :]
        junk = h[:, 1, :, :]

        names = ("w_loaded aneg_ready x_loaded var_ready rstd_ready xl_ready ssq_ready xr_ready ms_ready rrms_ready "
                 "xn_ready tp_done tp_evac in_done in_evac conv_done xs_ready xp_done dtr_ready bc_ready "
                 "bcd_written dtp_done resp_done a_evac sp_ready delta_ready du_ready z_evac da_ready "
                 "scan_done state_saved bquad_used cmul_done y_summed gated yg_ready op_done x1_ready x1_stored "
                 "norm_chain conv_chain act_chain sp_chain").split()
        S = {n: sem("m_" + n) for n in names}
        b_loaded = [sem(f"m_b_loaded{q}") for q in range(NQ)]
        c_loaded = [sem(f"m_c_loaded{q}") for q in range(NQ)]
        wslot = [sem(f"m_wslot{u}") for u in range(2)]

        loads = [(norm_w[:], bcast(dram.w_norm, [P, DM])), (w_in[:], dram.w_in_x), (conv_w[:], dram.conv_w),
                 (conv_b[:], dram.conv_b), (b_dt[:], dram.b_dt), (d_skip[:], dram.d_skip),
                 (a_neg[:], dram.a_log), (w_xp[:], dram.w_xp), (w_out[:], dram.w_out)]
        NW = 16 * len(loads)
        NORM_LINKS, CONV_LINKS, ACT_LINKS = 2 * ST + 1, DC * (KW + 1), 2

        def segments(eng, norm, body, after=lambda s, th: None):
            norm(0, 0)
            with eng.Fori(0, NB) as b:
                for th in range(HALVES):
                    s = b * HALVES + th
                    body(b, th, s)
                    norm(s + 1, 1 - th)
                    after(s, th)

        def chunks(eng, body):
            body(0, 0, True, False)
            with eng.Fori(0, (DC - 2) // 2) as r:
                for k in range(2):
                    body(r * 2 + (1 + k), (1 + k) % 2, False, False)
            body(DC - 1, (DC - 1) % 2, False, True)

        with nc.Block() as block:
            @block.sync
            def _(eng):
                eng.sem_inc(S["x1_stored"], 16)
                eng.dma_start(xin[:, 0], dram.x_seg[0]).then_inc(S["x_loaded"], 16)
                for dst, src in loads:
                    eng.dma_start(dst, src).then_inc(S["w_loaded"], 16)

                def load_x(s, half):
                    eng.dma_start(xin[:, half], dram.x_seg[bass.ds(s, 1)].rearrange("a p t n -> (a p) t n"))\
                        .then_inc(S["x_loaded"], 16)

                def segment(b, th, s):
                    def slot(d, u):
                        g = s * DC + d
                        eng.wait_ge(S["resp_done"], g + 1)
                        dd = bass.ds(d, 1)
                        eng.dma_start(w_res[:, u], dram.w_in_res[dd].rearrange("a p k n -> (a p) k n"))\
                            .then_inc(wslot[u], 16)
                        eng.dma_start(w_dt[:, u], dram.w_dt[dd].rearrange("a p n -> (a p) n")).then_inc(wslot[u], 16)

                    slot(0, 0)
                    slot(1, 1)
                    eng.wait_ge(S["bc_ready"], s + 1)
                    eng.dma_start(dram.bcd[bass.ds(s, 1)].rearrange("a n t -> (a n) t"), bc[:])\
                        .then_inc(S["bcd_written"], 16)
                    eng.wait_ge(S["bcd_written"], (s + 1) * 16)
                    for q in range(NQ):
                        for (dst, loaded, used, off) in ((b_rep, b_loaded, "bquad_used", 0), (c_rep, c_loaded, "cmul_done", NS)):
                            credit = {"bquad_used": DC * NQ, "cmul_done": DC * NQ}[used]
                            eng.wait_ge(S[used], s * (DC * NQ) - (NQ - 1 - q) + credit)
                            src = dram.bcd[bass.ds(s, 1), off + Q * q:off + Q * q + Q, :]
                            eng.dma_start(dst[:, Q * q:Q * q + Q, :], src.to_broadcast([P, Q, SEG]))\
                                .then_inc(loaded[q], 16)
                    eng.wait_ge(S["x1_stored"], s * (16 * ST) + 16)
                    load_x(b * HALVES + 1 if th == 0 else (b * -1 + 1) * HALVES, 1 - th)
                    with eng.Fori(0, (DC - 2) // 2) as r:
                        for k in range(2):
                            slot(r * 2 + (2 + k), k)
                    for i in range(ST):
                        eng.wait_ge(S["x1_ready"], s * ST + (i + 1))
                        eng.dma_start(dram.x1_seg[bass.ds(s, 1), :, i, :].rearrange("a p n -> (a p) n"), xin[:, th, i, :])\
                            .then_inc(S["x1_stored"], 16)

                segments(eng, lambda s, half: None, segment)
                eng.wait_ge(S["x1_stored"], 16 * TT + 16)

            @block.scalar
            def _(eng):
                eng.sem_inc(S["in_evac"], 2)
                eng.sem_inc(S["tp_evac"], 2)
                eng.sem_inc(S["a_evac"], 1)
                eng.sem_inc(S["z_evac"], 1)
                eng.sem_inc(S["xs_ready"], 2)
                eng.wait_ge(S["w_loaded"], NW)
                eng.activation(a_neg[:], a_neg[:], ACT.Exp).then_inc(S["aneg_ready"], 1)
                eng.wait_ge(S["aneg_ready"], 2)

                def norm(s, half):
                    ch = Chain(eng, S["act_chain"], s * ACT_LINKS)
                    eng.wait_ge(S["var_ready"], s + 1)
                    ch.add(eng.activation(rstd[:], var1[:], ACT.Ln))
                    ch.settle()
                    eng.activation(rstd[:], rstd[:], ACT.Exp, scale=-0.5).then_inc(S["rstd_ready"], 1)
                    for i in range(ST):
                        eng.wait_ge(S["xl_ready"], s * ST + (i + 1))
                        eng.activation(junk[:, i, :], xl[:, i, :], ACT.Square, accum_out=ssq[:, i:i + 1])\
                            .then_inc(S["ssq_ready"], 1)
                    eng.wait_ge(S["ms_ready"], s + 1)
                    ch.add(eng.activation(rrms[:], ms[:], ACT.Ln))
                    ch.settle()
                    eng.activation(rrms[:], rrms[:], ACT.Exp, scale=-0.5).then_inc(S["rrms_ready"], 1)
                    for i in range(ST):
                        eng.wait_ge(S["tp_done"], s * ST + (i + 1))
                        eng.activation(xnT[:, :, i * P:(i + 1) * P],
                                       bank[6 + i % 2][:].rearrange("p (k t) -> p k t", k=KC), ACT.Copy)\
                            .then_inc(S["tp_evac"], 1)
                    assert ch.n == ACT_LINKS, ch.n

                def segment(b, th, s):
                    def silu(d):
                        eng.wait_ge(S["conv_done"], s * DC + (d + 1 + 2))
                        eng.activation(xs[:, d, :], cv[:, d % 2, :], ACT.Silu).then_inc(S["xs_ready"], 1)

                    for d in range(DC):
                        eng.wait_ge(S["in_done"], s * DC + (d + 1))
                        eng.wait_ge(S["conv_done"], s * DC + (d + 1))
                        eng.activation(xraw[:, d % 2, KW - 1:], bank[4 + d % 2][:], ACT.Copy).then_inc(S["in_evac"], 1)
                        if d:
                            silu(d - 1)
                    silu(DC - 1)
                    eng.wait_ge(S["xp_done"], s + 1)
                    eng.activation(dtr[:], bank[6][:], ACT.Copy).then_inc(S["dtr_ready"], 1)
                    eng.activation(bc[:], bank[7][0:2 * NS, :], ACT.Copy).then_inc(S["bc_ready"], 1)

                    def prep_a(d, u):
                        g = s * DC + d
                        eng.wait_ge(S["dtp_done"], g + 1)
                        eng.wait_ge(S["du_ready"], g + 1)
                        eng.activation(delta[:, u, :], bank[7][:], ACT.Identity, bias=b_dt[:, bass.ds(d, 1)])\
                            .then_inc(S["a_evac"], 1)
                        eng.wait_ge(S["a_evac"], g + 2)
                        eng.activation(spl[:, u, :], delta[:, u, :], ACT.Abs).then_inc(S["sp_chain"], 1)

                    def prep_b(d, u):
                        g = s * DC + d
                        eng.wait_ge(S["sp_chain"], g * 2 + 1)
                        eng.activation(spl[:, u, :], spl[:, u, :], ACT.Exp, scale=-1.0).then_inc(S["sp_chain"], 1)
                        eng.wait_ge(S["sp_chain"], g * 2 + 2)
                        eng.activation(spl[:, u, :], spl[:, u, :], ACT.Ln, bias=c.ones[:, 0:1])\
                            .then_inc(S["sp_ready"], 1)

                    def prep_c(d, u):
                        g = s * DC + d
                        eng.wait_ge(S["resp_done"], g + 1 + 2)
                        eng.wait_ge(S["yg_ready"], g + 1)
                        eng.activation(zs[:, u, :], bank[7][:], ACT.Silu).then_inc(S["z_evac"], 1)

                    prep_a(0, 0)
                    prep_b(0, 0)
                    prep_c(0, 0)

                    def chunk(d, u, first, last):
                        g = s * DC + d
                        eng.wait_ge(S["delta_ready"], g + 1)
                        for q in range(NQ):
                            for j in range(Q):
                                eng.wait_ge(S["scan_done"], g * NS + (q * Q + j + 1))
                                eng.activation(bank[j][:], delta[:, u, :], ACT.Exp,
                                               scale=a_neg[:, bass.ds(d * NS + (q * Q + j), 1)]).then_inc(S["da_ready"], 1)
                            if not last and q == 1:
                                prep_a(d + 1, 1 - u)
                            if not last and q == 2:
                                prep_b(d + 1, 1 - u)
                            if not last and q == 3:
                                prep_c(d + 1, 1 - u)

                    chunks(eng, chunk)

                segments(eng, norm, segment)

            @block.vector
            def _(eng):
                eng.sem_inc(S["scan_done"], Q)
                eng.sem_inc(S["bquad_used"], DC * NQ)
                eng.sem_inc(S["du_ready"], 2)
                eng.sem_inc(S["yg_ready"], 2)
                eng.sem_inc(S["conv_done"], 2)
                eng.wait_ge(S["w_loaded"], NW)
                eng.wait_ge(S["aneg_ready"], 1)
                eng.tensor_scalar(a_neg[:], a_neg[:], -1.0, None, ALU.mult).then_inc(S["aneg_ready"], 1)

                def norm(s, half):
                    ch = Chain(eng, S["norm_chain"], s * NORM_LINKS)
                    eng.wait_ge(S["x_loaded"], (s + 1) * 16)
                    for i in range(ST):
                        ch.add(eng.bn_stats(st6[:, i, :], xin[:, half, i, :]))
                    ch.settle()
                    ch.add(eng.memset(var1[:], 0.0))
                    for i in range(ST):
                        ch.add(eng.bn_aggr(mv[:, i, :], st6[:, i, :]))
                    ch.settle()
                    eng.tensor_scalar(var1[:], mv[:, :, 1], EPS_LN, None, ALU.add).then_inc(S["var_ready"], 1)
                    eng.wait_ge(S["rstd_ready"], s + 1)
                    for i in range(ST):
                        eng.tensor_scalar(xl[:, i, :], xin[:, half, i, :], mv[:, i, 0:1], rstd[:, i:i + 1],
                                          ALU.subtract, ALU.mult).then_inc(S["xl_ready"], 1)
                    eng.wait_ge(S["ssq_ready"], (s + 1) * ST)
                    eng.tensor_scalar(ms[:], ssq[:], 1.0 / DM, EPS_RMS_A, ALU.mult, ALU.add).then_inc(S["ms_ready"], 1)
                    eng.wait_ge(S["rrms_ready"], s + 1)
                    eng.wait_ge(S["xr_ready"], (s + 1) * ST)
                    for i in range(ST):
                        eng.scalar_tensor_tensor(xl[:, i, :], xl[:, i, :], rrms[:, i:i + 1], norm_w[:],
                                                 ALU.mult, ALU.mult).then_inc(S["xn_ready"], 1)
                    assert ch.n == NORM_LINKS, ch.n

                def segment(b, th, s):
                    ch = Chain(eng, S["conv_chain"], s * CONV_LINKS)
                    for d in range(DC):
                        x = xraw[:, d % 2, :]
                        if th == 0:
                            ch.add(eng.memset(x[:, 0:KW - 1], 0.0))
                        else:
                            ch.add(eng.tensor_copy(x[:, 0:KW - 1], hist[:, d, :]))
                        eng.wait_ge(S["in_evac"], s * DC + (d + 1 + 2))
                        eng.wait_ge(S["xs_ready"], s * DC + (d + 1))
                        ch.settle()
                        y = cv[:, d % 2, :]
                        ch.add(eng.tensor_scalar(y, x[:, KW - 1:], conv_w[:, d, KW - 1:KW], conv_b[:, d:d + 1],
                                                 ALU.mult, ALU.add))
                        for k in range(KW - 2, -1, -1):
                            ch.settle()
                            ins = eng.scalar_tensor_tensor(y, x[:, k:k + SEG], conv_w[:, d, k:k + 1], y, ALU.mult, ALU.add)
                            if k:
                                ch.add(ins)
                            else:
                                ch.add(ins)
                                eng.tensor_copy(hist[:, d, :], x[:, SEG:SEG + KW - 1]).then_inc(S["conv_done"], 1)

                    def softplus(d, u):
                        g = s * DC + d
                        eng.wait_ge(S["sp_ready"], g + 1)
                        eng.scalar_tensor_tensor(delta[:, u, :], delta[:, u, :], 0.0, spl[:, u, :], ALU.max, ALU.add)\
                            .then_inc(S["delta_ready"], 1)

                    def delta_x(d, u):
                        g = s * DC + d
                        eng.wait_ge(S["delta_ready"], g + 1)
                        eng.wait_ge(S["bquad_used"], g * NQ + DC * NQ)
                        eng.tensor_tensor(bank[6][:], delta[:, u, :], xs[:, bass.ds(d, 1), :].rearrange("p a t -> p (a t)"),
                                          ALU.mult).then_inc(S["du_ready"], 1)

                    def gating(d, u):
                        g = s * DC + d
                        x = xs[:, bass.ds(d, 1), :].rearrange("p a t -> p (a t)")
                        eng.wait_ge(S["y_summed"], g * NQ + (NQ + NQ))
                        eng.scalar_tensor_tensor(bank[4 + u][:], x, d_skip[:, bass.ds(d, 1)], bank[4 + u][:],
                                                 ALU.mult, ALU.add).then_inc(S["gated"], 1)
                        eng.wait_ge(S["gated"], g + 1)
                        eng.wait_ge(S["z_evac"], g + 1 + 1)
                        eng.tensor_tensor(x, bank[4 + u][:], zs[:, u, :], ALU.mult).then_inc(S["yg_ready"], 1)

                    softplus(0, 0)
                    delta_x(0, 0)

                    def chunk(d, u, first, last):
                        g = s * DC + d
                        for q in range(NQ):
                            G = g * NQ + q
                            if first:
                                eng.wait_ge(b_loaded[q], (s + 1) * 16)
                            if q == 0:
                                eng.wait_ge(S["du_ready"], g + (1 + 2))
                            eng.wait_ge(S["y_summed"], G + 1)
                            eng.tensor_tensor(h[:, q], bank[6][:].unsqueeze(1).to_broadcast([P, Q, SEG]),
                                              b_rep[:, Q * q:Q * q + Q, :], ALU.mult).then_inc(S["bquad_used"], 1)
                            eng.wait_ge(S["bquad_used"], G + (1 + DC * NQ))
                            if not last and q == NQ - 1:
                                softplus(d + 1, 1 - u)
                                delta_x(d + 1, 1 - u)
                            for j in range(Q):
                                eng.wait_ge(S["da_ready"], g * NS + (q * Q + j + 1))
                                init = 0.0 if th == 0 else state[:, bass.ds(d * NS + (q * Q + j), 1)]
                                eng.tensor_tensor_scan(h[:, q, j, :], bank[j][:], h[:, q, j, :], init,
                                                       ALU.mult, ALU.add).then_inc(S["scan_done"], 1)
                            if not first and q == 1:
                                gating(d - 1, 1 - u)

                    chunks(eng, chunk)
                    gating(DC - 1, (DC - 1) % 2)
                    assert ch.n == CONV_LINKS, ch.n

                def residual(s, th):
                    for i in range(ST):
                        eng.wait_ge(S["op_done"], s * ST + (i + 1))
                        eng.tensor_tensor(xin[:, th, i, :], xin[:, th, i, :], bank[i][:], ALU.add)\
                            .then_inc(S["x1_ready"], 1)

                segments(eng, norm, segment, residual)

            @block.gpsimd
            def _(eng):
                eng.sem_inc(S["cmul_done"], DC * NQ)

                def norm(s, half):
                    for i in range(ST):
                        eng.wait_ge(S["xl_ready"], s * ST + (i + 1))
                        x = xin[:, half, i, :]
                        eng.tensor_tensor(x, x, xl[:, i, :], ALU.add).then_inc(S["xr_ready"], 1)

                def segment(b, th, s):
                    def chunk(d, u, first, last):
                        g = s * DC + d
                        for q in range(NQ):
                            G = g * NQ + q
                            if first:
                                eng.wait_ge(c_loaded[q], (s + 1) * 16)
                            eng.wait_ge(S["scan_done"], g * NS + (q * Q + Q + Q))
                            if th == 0:
                                eng.tensor_tensor(state[:, bass.ds(d * NS + q * Q, Q)], h[:, q, :, SEG - 1], c.ones[:, 0:Q],
                                                  ALU.mult).then_inc(S["state_saved"], 1)
                                eng.wait_ge(S["state_saved"], b * (DC * NQ) + d * NQ + (q + 1))
                            eng.tensor_tensor(h[:, q], h[:, q], c_rep[:, Q * q:Q * q + Q, :], ALU.mult)\
                                .then_inc(S["cmul_done"], 1)

                    chunks(eng, chunk)

                segments(eng, norm, segment)

            @block.tensor
            def _(eng):
                eng.sem_inc(S["resp_done"], 2)
                eng.sem_inc(S["y_summed"], NQ)
                eng.wait_ge(S["w_loaded"], NW)

                def norm(s, half):
                    for i in range(ST):
                        eng.wait_ge(S["xn_ready"], s * ST + (i + 1))
                        eng.wait_ge(S["tp_evac"], s * ST + (i + 1))
                        for k in range(KC):
                            ins = eng.transpose(bank[6 + i % 2][:, k * P:(k + 1) * P], xl[:, i, k * P:(k + 1) * P], c.ident[:])
                        ins.then_inc(S["tp_done"], 1)

                def segment(b, th, s):
                    eng.wait_ge(S["tp_evac"], s * ST + (ST + 2))
                    for d in range(DC):
                        eng.wait_ge(S["in_evac"], s * DC + (d + 1))
                        for k in range(KC):
                            ins = eng.matmul(bank[4 + d % 2][:], w_in[:, k, d * P:(d + 1) * P], xnT[:, k, :],
                                             start=(k == 0), stop=(k == KC - 1))
                        ins.then_inc(S["in_done"], 1)
                    for d in range(DC):
                        eng.wait_ge(S["xs_ready"], s * DC + (d + 1 + 2))
                        eng.matmul(bank[6][:], w_xp[:, d, 0:DR], xs[:, d, :], start=(d == 0), stop=(d == DC - 1))
                        ins = eng.matmul(bank[7][0:2 * NS, :], w_xp[:, d, DR:], xs[:, d, :], start=(d == 0), stop=(d == DC - 1))
                    ins.then_inc(S["xp_done"], 1)
                    eng.wait_ge(S["dtr_ready"], s + 1)
                    eng.wait_ge(S["bc_ready"], s + 1)
                    eng.wait_ge(S["in_evac"], s * DC + (DC + 2))

                    def prep(d, u, uses):
                        g = s * DC + d
                        eng.wait_ge(wslot[u], (s * (DC // 2) + uses) * 32)
                        eng.wait_ge(S["z_evac"], g + 1)
                        eng.matmul(bank[7][:], w_dt[:, u, :], dtr[:], start=True, stop=True).then_inc(S["dtp_done"], 1)
                        eng.wait_ge(S["a_evac"], g + 2)
                        for k in range(KC):
                            ins = eng.matmul(bank[7][:], w_res[:, u, k, :], xnT[:, k, :], start=(k == 0), stop=(k == KC - 1))
                        ins.then_inc(S["resp_done"], 1)

                    prep(0, 0, 1)

                    def chunk(d, u, first, last):
                        g = s * DC + d
                        if not last:
                            prep(d + 1, 1 - u, 1 if first else pos["r"] + 2)
                        eng.wait_ge(S["yg_ready"], g + 1)
                        for q in range(NQ):
                            G = g * NQ + q
                            eng.wait_ge(S["cmul_done"], G + (1 + DC * NQ))
                            for j in range(Q):
                                ins = eng.matmul(bank[4 + u][:], c.ident[:], h[:, q, j, :],
                                                 start=(q == 0 and j == 0), stop=(q == NQ - 1 and j == Q - 1))
                            ins.then_inc(S["y_summed"], 1)

                    pos = {}

                    chunk(0, 0, True, False)
                    with eng.Fori(0, (DC - 2) // 2) as r:
                        pos["r"] = r
                        for k in range(2):
                            chunk(r * 2 + (1 + k), (1 + k) % 2, False, False)
                    chunk(DC - 1, (DC - 1) % 2, False, True)

                    eng.wait_ge(S["yg_ready"], s * DC + (DC + 2))
                    eng.wait_ge(S["z_evac"], s * DC + (DC + 1))
                    for i in range(ST):
                        for d in range(DC):
                            ins = eng.matmul(bank[i][:], xs[:, d, i * P:(i + 1) * P], w_out[:, d, :],
                                             start=(d == 0), stop=(d == DC - 1))
                        ins.then_inc(S["op_done"], 1)

                segments(eng, norm, segment)


def tokens(nc, c, dram):
    ctx = ExitStack()
    with ctx:
        def sb(name, shape, dt=F32):
            return ctx.enter_context(nc.sbuf_tensor(name, shape, dt))

        bank = [ctx.enter_context(nc.psum_tensor(f"tbank{i}", [P, 512], F32)) for i in range(8)]
        norm_w = sb("norm_w_f", [P, DM])
        w_r = sb("w_router", [P, KC, E])
        w_g, w_u, w_d = sb("w_sg", [P, KC, SH]), sb("w_su", [P, KC, SH]), sb("w_sd", [P, SH // P, DM])
        x1 = sb("x1_group", [P, ST, DM])
        xl = sb("xl_group", [P, ST, DM])
        flat = sb("flat_group", [P, ST, DM])
        junk = sb("square_group", [P, ST, DM])
        flT = sb("flat_T", [P, ST, KC, P])
        gs = sb("gate_silu", [P, 2, SH])
        act = sb("act_shared", [P, 2, SH])
        actT = sb("act_shared_T", [P, 2, SH // P, P])
        st6, mv = sb("f_st6", [P, ST, 6]), sb("f_mv", [P, ST, 2])
        var1, rstd = sb("f_var", [P, ST]), sb("f_rstd", [P, ST])
        ssq, ms, rrms = sb("f_ssq", [P, ST]), sb("f_ms", [P, ST]), sb("f_rrms", [P, ST])
        names = ("w_loaded x_loaded var_ready rstd_ready xl_ready ssq_ready base_ready ms_ready rrms_ready flat_ready "
                 "tp_done tp_evac gu_done silu_done act_ready at_done at_evac sd_done sd_added logits_done "
                 "logits_read dve_chain act_chain").split()
        S = {n: ctx.enter_context(nc.semaphore("t_" + n)) for n in names}
        loads = [(norm_w[:], bcast(dram.norm_w, [P, DM])), (w_r[:], dram.router_w), (w_g[:], dram.sg),
                 (w_u[:], dram.su), (w_d[:], dram.sd)]
        NG = TT // ST
        DVE_LINKS = 2 * ST + 1

        def skewed(eng, norm, work):
            norm(0)
            with eng.Fori(0, NG - 1) as r:
                norm(r + 1)
                work(r)
            work(NG - 1)

        with nc.Block() as block:
            @block.sync
            def _(eng):
                for dst, src in loads[:1]:
                    eng.dma_start(dst, src).then_inc(S["w_loaded"], 16)

                def load(g):
                    eng.dma_start(x1[:], dram.x1_seg[bass.ds(g, 1)].rearrange("a p t n -> (a p) t n"))\
                        .then_inc(S["x_loaded"], 16)

                def store(g):
                    eng.wait_ge(S["flat_ready"], g * ST + ST)
                    eng.dma_start(dram.flat_seg[bass.ds(g, 1)].rearrange("a p t n -> (a p) t n"), flat[:])\
                        .then_inc(c.flat_stored, 16)

                load(0)
                for dst, src in loads[1:]:
                    eng.dma_start(dst, src).then_inc(S["w_loaded"], 16)
                for e in range(RING):
                    eng.dma_start(c.w1r[:, e], dram.w1[e]).then_inc(c.w_landed[e], 16)
                    eng.dma_start(c.w2r[:, e], dram.w2[e]).then_inc(c.w_landed[e], 16)
                with eng.Fori(0, NG - 1) as r:
                    eng.wait_ge(S["base_ready"], r * ST + ST)
                    eng.wait_ge(S["xl_ready"], r * ST + ST)
                    load(r + 1)
                    store(r)
                store(NG - 1)
                eng.wait_ge(c.flat_stored, 16 * NG)

            @block.scalar
            def _(eng):
                eng.sem_inc(S["tp_evac"], 2)
                eng.sem_inc(S["at_evac"], 1)

                def norm(g):
                    ch = Chain(eng, S["act_chain"], g * 2)
                    eng.wait_ge(S["var_ready"], g + 1)
                    ch.add(eng.activation(rstd[:], var1[:], ACT.Ln))
                    ch.settle()
                    eng.activation(rstd[:], rstd[:], ACT.Exp, scale=-0.5).then_inc(S["rstd_ready"], 1)
                    for i in range(ST):
                        eng.wait_ge(S["xl_ready"], g * ST + (i + 1))
                        eng.activation(junk[:, i, :], xl[:, i, :], ACT.Square, accum_out=ssq[:, i:i + 1])\
                            .then_inc(S["ssq_ready"], 1)
                    eng.wait_ge(S["ms_ready"], g + 1)
                    ch.add(eng.activation(rrms[:], ms[:], ACT.Ln))
                    ch.settle()
                    eng.activation(rrms[:], rrms[:], ACT.Exp, scale=-0.5).then_inc(S["rrms_ready"], 1)

                def work(g):
                    def transposed(i):
                        eng.wait_ge(S["tp_done"], g * ST + (i + 1))
                        eng.activation(flT[:, i], bank[i % 2][:].rearrange("p (k t) -> p k t", k=KC), ACT.Copy)\
                            .then_inc(S["tp_evac"], 1)

                    def silu(i):
                        eng.wait_ge(S["gu_done"], g * ST + (i + 1))
                        eng.wait_ge(S["act_ready"], g * ST + (i + 1))
                        eng.activation(gs[:, i % 2], bank[3 + 2 * (i % 2)][:], ACT.Silu).then_inc(S["silu_done"], 1)

                    def act_transposed(i):
                        eng.wait_ge(S["at_done"], g * ST + (i + 1 + 2))
                        eng.wait_ge(S["sd_done"], g * ST + (i + 1))
                        eng.activation(actT[:, i % 2], bank[7][:].rearrange("p (k t) -> p k t", k=SH // P), ACT.Copy)\
                            .then_inc(S["at_evac"], 1)

                    transposed(0), transposed(1), silu(0), transposed(2), silu(1), transposed(3)
                    act_transposed(0), silu(2), act_transposed(1), silu(3), act_transposed(2), act_transposed(3)

                skewed(eng, norm, work)

            @block.vector
            def _(eng):
                eng.sem_inc(S["act_ready"], 2)
                eng.sem_inc(S["sd_added"], 2)
                eng.sem_inc(S["logits_read"], 1)
                eng.wait_ge(S["w_loaded"], 16 * len(loads))

                def norm(g):
                    ch = Chain(eng, S["dve_chain"], g * DVE_LINKS)
                    eng.wait_ge(S["x_loaded"], g * 16 + 16)
                    for i in range(ST):
                        ch.add(eng.bn_stats(st6[:, i, :], x1[:, i, :]))
                    ch.settle()
                    ch.add(eng.memset(var1[:], 0.0))
                    for i in range(ST):
                        ch.add(eng.bn_aggr(mv[:, i, :], st6[:, i, :]))
                    ch.settle()
                    eng.tensor_scalar(var1[:], mv[:, :, 1], EPS_LN, None, ALU.add).then_inc(S["var_ready"], 1)
                    eng.wait_ge(S["rstd_ready"], g + 1)
                    for i in range(ST):
                        eng.tensor_scalar(xl[:, i, :], x1[:, i, :], mv[:, i, 0:1], rstd[:, i:i + 1],
                                          ALU.subtract, ALU.mult).then_inc(S["xl_ready"], 1)
                    eng.wait_ge(S["ssq_ready"], g * ST + ST)
                    eng.tensor_scalar(ms[:], ssq[:], 1.0 / DM, EPS_RMS_F, ALU.mult, ALU.add).then_inc(S["ms_ready"], 1)
                    eng.wait_ge(S["rrms_ready"], g + 1)
                    eng.wait_ge(S["tp_done"], g * ST + 0) if not isinstance(g, int) else None
                    eng.wait_ge(c.flat_stored, g * 16) if not isinstance(g, int) else None
                    for i in range(ST):
                        eng.scalar_tensor_tensor(flat[:, i, :], xl[:, i, :], rrms[:, i:i + 1], norm_w[:],
                                                 ALU.mult, ALU.mult).then_inc(S["flat_ready"], 1)
                    assert ch.n == DVE_LINKS, ch.n

                def work(g):
                    def mult(i):
                        eng.wait_ge(S["silu_done"], g * ST + (i + 1))
                        eng.wait_ge(S["at_done"], g * ST + (i + 1))
                        eng.tensor_tensor(act[:, i % 2], gs[:, i % 2], bank[4 + 2 * (i % 2)][:], ALU.mult)\
                            .then_inc(S["act_ready"], 1)

                    def add(i):
                        eng.wait_ge(S["sd_done"], g * ST + (i + 1 + 2))
                        eng.wait_ge(S["base_ready"], g * ST + (i + 1))
                        b = c.base[:, bass.ds(g * ST + i, 1), :].rearrange("p a n -> p (a n)")
                        eng.tensor_tensor(b, b, bank[i % 2][:], ALU.add).then_inc(S["sd_added"], 1)

                    mult(0), mult(1), add(0), mult(2), add(1), mult(3), add(2)
                    eng.wait_ge(S["logits_done"], g + 1)
                    eng.tensor_scalar(c.logits[:, bass.ds(g * ST, ST), :], bank[2][:, 0:ST * E].rearrange("p (t e) -> p t e", t=ST),
                                      0.0, None, ALU.add).then_inc(S["logits_read"], 1)
                    add(3)

                skewed(eng, norm, work)

            @block.gpsimd
            def _(eng):
                with eng.Fori(0, NG) as g:
                    for i in range(ST):
                        eng.wait_ge(S["xl_ready"], g * ST + (i + 1))
                        eng.tensor_tensor(c.base[:, bass.ds(g * ST + i, 1), :].rearrange("p a n -> p (a n)"),
                                          x1[:, i, :], xl[:, i, :], ALU.add).then_inc(S["base_ready"], 1)

            @block.tensor
            def _(eng):
                eng.sem_inc(S["at_done"], 2)
                eng.sem_inc(S["sd_done"], 2)
                eng.wait_ge(S["w_loaded"], 16 * len(loads))

                with eng.Fori(0, NG) as g:
                    def transposes(i):
                        eng.wait_ge(S["flat_ready"], g * ST + (i + 1))
                        if i < 2:
                            eng.wait_ge(S["sd_added"], g * ST + (i + 1))
                        eng.wait_ge(S["tp_evac"], g * ST + (i + 1))
                        for k in range(KC):
                            ins = eng.transpose(bank[i % 2][:, k * P:(k + 1) * P], flat[:, i, k * P:(k + 1) * P], c.ident[:])
                        ins.then_inc(S["tp_done"], 1)

                    def gate_up(i):
                        eng.wait_ge(S["tp_evac"], g * ST + (i + 1 + 2))
                        if i == 0:
                            eng.wait_ge(S["logits_read"], g + 1)
                        for k in range(KC):
                            ins = eng.matmul(bank[2][:, i * E:(i + 1) * E], flT[:, i, k, :], w_r[:, k, :],
                                             start=(k == 0), stop=(k == KC - 1))
                        if i == ST - 1:
                            ins.then_inc(S["logits_done"], 1)
                        eng.wait_ge(S["act_ready"], g * ST + (i + 1))
                        for w, o in ((w_g, 3), (w_u, 4)):
                            for k in range(KC):
                                ins = eng.matmul(bank[o + 2 * (i % 2)][:], flT[:, i, k, :], w[:, k, :],
                                                 start=(k == 0), stop=(k == KC - 1))
                        ins.then_inc(S["gu_done"], 1)

                    def down(i):
                        eng.wait_ge(S["act_ready"], g * ST + (i + 1 + 2))
                        eng.wait_ge(S["at_evac"], g * ST + (i + 1))
                        for k in range(SH // P):
                            ins = eng.transpose(bank[7][:, k * P:(k + 1) * P], act[:, i % 2, k * P:(k + 1) * P], c.ident[:])
                        ins.then_inc(S["at_done"], 1)
                        eng.wait_ge(S["at_evac"], g * ST + (i + 1 + 1))
                        eng.wait_ge(S["sd_added"], g * ST + (i + 1))
                        for k in range(SH // P):
                            ins = eng.matmul(bank[i % 2][:], actT[:, i % 2, k, :], w_d[:, k, :],
                                             start=(k == 0), stop=(k == SH // P - 1))
                        ins.then_inc(S["sd_done"], 1)

                    transposes(0), transposes(1), gate_up(0), transposes(2), gate_up(1), transposes(3)
                    eng.wait_ge(S["tp_evac"], g * ST + (ST + 2))
                    down(0), gate_up(2), down(1), gate_up(3), down(2), down(3)


def routing(nc, c, dram):
    ctx = ExitStack()
    with ctx:
        def sb(name, shape, dt=F32):
            return ctx.enter_context(nc.sbuf_tensor(name, shape, dt))

        rank_ps = ctx.enter_context(nc.psum_tensor("rank_ps", [P, TT * E], F32))
        count_ps = ctx.enter_context(nc.psum_tensor("count_ps", [P, 512], F32))
        list_ps = ctx.enter_context(nc.psum_tensor("list_ps", [P, 512], F32))
        mx, sm = sb("mx", [P, TT]), sb("sm", [P, TT])
        prob = sb("prob", [P, TT, E])
        top = sb("top", [P, TT, 8])
        top_i = sb("top_i", [P, TT, 8], U32)
        idx = sb("idx", [P, TT, TOPK])
        oh = sb("oh", [P, TOPK, TT, E])
        mask, cum = sb("mask", [P, TT, E]), sb("cum", [P, TT + 1, E])
        cnt, nt, end, zero = sb("cnt", [P, E]), sb("nt", [P, E]), sb("end", [P, E]), sb("zero", [P, E])
        off = sb("off", [P, E])
        NM = T // P
        cmp = sb("cmp", [P, E, NM])
        posn, hit = sb("posn", [P, TT, E]), sb("hit", [P, TT, E])
        lo_i, hi_i = sb("lo_i", [P, TT * TOPK], I32), sb("hi_i", [P, TT * TOPK], I32)
        dest_i = sb("dest_i", [P, TT * TOPK], I32)
        lo, hi = sb("lo", [P, TT * TOPK]), sb("hi", [P, TT * TOPK])
        iota_i, iota = sb("iota_i", [P, P], I32), sb("iota", [P, P])
        tok_i, tok = sb("tok_i", [P, TT], I32), sb("tok", [P, TT])
        thr_i, thr = sb("thr_i", [P, NM], I32), sb("thr", [P, NM])
        oh_lo, oh_hi = sb("oh_lo", [P, TOPK, P]), sb("oh_hi", [P, TOPK, NT])
        ecmp, etile = sb("ecmp", [1, NT, E]), sb("etile", [1, NT])
        names = "iota_made chain max_ready exp_done mask_ready counted hot_ready placed listed".split()
        S = {n: ctx.enter_context(nc.semaphore("r_" + n)) for n in names}

        with nc.Block() as block:
            @block.gpsimd
            def _(eng):
                eng.iota(iota_i[:], pattern=[[1, P]], base=0, channel_multiplier=0).then_inc(S["iota_made"], 1)
                eng.iota(tok_i[:], pattern=[[P, TT]], base=0, channel_multiplier=1).then_inc(S["iota_made"], 1)
                eng.iota(thr_i[:], pattern=[[P, NM]], base=0, channel_multiplier=0).then_inc(S["iota_made"], 1)

            @block.scalar
            def _(eng):
                eng.wait_ge(S["max_ready"], 1)
                eng.activation(prob[:], prob[:], ACT.Exp).then_inc(S["exp_done"], 1)

            @block.vector
            def _(eng):
                ch = Chain(eng, S["chain"])
                row = lambda ap, n: ap.unsqueeze(2).to_broadcast([P, ap.shape[1], n])
                ch.add(eng.tensor_reduce(mx[:], c.logits[:], AX.X, ALU.max))
                ch.settle()
                eng.tensor_tensor(prob[:], c.logits[:], row(mx[:], E), ALU.subtract).then_inc(S["max_ready"], 1)
                eng.wait_ge(S["iota_made"], 3)
                for a, b in ((iota, iota_i), (tok, tok_i), (thr, thr_i)):
                    ch.add(eng.tensor_copy(a[:], b[:]))
                ch.add(eng.memset(zero[:], 0.0))
                ch.add(eng.memset(cum[:, 0, :], 0.0))
                ch.add(eng.memset(c.dest[:, TT:, :], 0.0))
                ch.add(eng.memset(c.slot_token[:, NT:], 0.0))
                eng.wait_ge(S["exp_done"], 1)
                ch.add(eng.tensor_reduce(sm[:], prob[:], AX.X, ALU.add))
                ch.settle()
                ch.add(eng.reciprocal(sm[:], sm[:]))
                ch.settle()
                ch.add(eng.tensor_tensor(prob[:], prob[:], row(sm[:], E), ALU.mult))
                ch.settle()
                for t in range(TT):
                    ch.add(eng.max(top[:, t, :], prob[:, t, :]))
                ch.settle()
                for t in range(TT):
                    ch.add(eng.max_index(top_i[:, t, :], top[:, t, :], prob[:, t, :]))
                ch.add(eng.tensor_reduce(sm[:], top[:, :, 0:TOPK], AX.X, ALU.add))
                ch.settle()
                ch.add(eng.reciprocal(sm[:], sm[:]))
                ch.add(eng.tensor_copy(idx[:], top_i[:, :, 0:TOPK]))
                ch.settle()
                ch.add(eng.tensor_tensor(c.weight[:], top[:, :, 0:TOPK], row(sm[:], TOPK), ALU.mult))
                ex = iota[:, 0:E].unsqueeze(1).to_broadcast([P, TT, E])
                for k in range(TOPK):
                    ch.add(eng.tensor_tensor(oh[:, k], ex, row(idx[:, :, k], E), ALU.is_equal))
                ch.settle()
                ch.add(eng.tensor_tensor(mask[:], oh[:, 0], oh[:, 1], ALU.add))
                ch.add(eng.tensor_tensor(hit[:], oh[:, 2], oh[:, 3], ALU.add))
                ch.settle()
                ch.add(eng.tensor_tensor(mask[:], mask[:], hit[:], ALU.add))
                for t in range(TT):
                    ch.settle()
                    ch.add(eng.tensor_tensor(cum[:, t + 1, :], cum[:, t, :], mask[:, t, :], ALU.add))
                ch.settle()
                eng.memset(hit[:], 0.0).then_inc(S["mask_ready"], 1)
                eng.wait_ge(S["counted"], 1)
                ch.add(eng.tensor_copy(cnt[:], count_ps[:, 0:E]))
                ch.settle()
                ch.add(eng.tensor_tensor(cmp[:], row(cnt[:], NM), thr[:].unsqueeze(1).to_broadcast([P, E, NM]), ALU.is_gt))
                ch.settle()
                ch.add(eng.tensor_reduce(nt[:], cmp[:], AX.X, ALU.add))
                ch.settle()
                ch.add(eng.tensor_tensor_scan(end[:], nt[:], zero[:], 0.0, ALU.add, ALU.add))
                ch.settle()
                ch.add(eng.tensor_tensor(off[:], end[:], nt[:], ALU.subtract))
                ch.settle()
                ch.add(eng.tensor_scalar(off[:], off[:], float(P), None, ALU.mult))
                ch.settle()
                ch.add(eng.tensor_tensor(posn[:], rank_ps[:].rearrange("p (t e) -> p t e", t=TT),
                                         off[:].unsqueeze(1).to_broadcast([P, TT, E]), ALU.add))
                for k in range(TOPK):
                    ch.settle()
                    ch.add(eng.tensor_tensor(hit[:], oh[:, k], posn[:], ALU.mult))
                    ch.settle()
                    ch.add(eng.tensor_reduce(c.dest[:, 0:TT, k], hit[:], AX.X, ALU.add))
                ch.settle()
                flat_dest = c.dest[:, 0:TT, :].rearrange("p t k -> p (t k)")
                ch.add(eng.tensor_copy(dest_i[:], flat_dest))
                ch.settle()
                ch.add(eng.tensor_scalar(lo_i[:], dest_i[:], P - 1, None, ALU.bitwise_and))
                ch.add(eng.tensor_scalar(hi_i[:], dest_i[:], P.bit_length() - 1, None, ALU.arith_shift_right))
                ch.settle()
                ch.add(eng.tensor_copy(lo[:], lo_i[:]))
                ch.add(eng.tensor_copy(hi[:], hi_i[:]))
                ch.settle()
                ch.add(eng.tensor_tensor(ecmp[:], end[0:1, :].unsqueeze(1).to_broadcast([1, NT, E]),
                                         iota[0:1, 0:NT].unsqueeze(2).to_broadcast([1, NT, E]), ALU.is_le))
                ch.settle()
                ch.add(eng.tensor_reduce(etile[:], ecmp[:], AX.X, ALU.add))
                ch.settle()
                ch.add(eng.tensor_scalar(etile[:], etile[:], float(E - 1), None, ALU.min))
                ch.settle()
                ch.add(eng.tensor_scalar(c.tile_need[:], etile[:], 1.0, None, ALU.add))
                ch.add(eng.tensor_copy(c.tile_ring[:], etile[:]))
                ch.add(eng.tensor_scalar(c.expert_end[:], end[0:1, :], 1.0, None, ALU.add))
                ch.settle()
                ch.add(eng.tensor_scalar(c.tile_ring[:], c.tile_ring[:], RING - 1, None, ALU.bitwise_and))
                eng.sem_inc(S["placed"], 1)
                with eng.Fori(0, TT) as t:
                    for k in range(TOPK):
                        at = bass.ds(t * TOPK + k, 1)
                        eng.wait_ge(S["placed"], t * TOPK + (k + 1))
                        eng.tensor_scalar(oh_lo[:, k], iota[:], lo[:, at], None, ALU.is_equal).then_inc(S["hot_ready"], 1)
                        eng.tensor_scalar(oh_hi[:, k], iota[:, 0:NT], hi[:, at], tok[:, bass.ds(t, 1)], ALU.is_equal,
                                          ALU.mult).then_inc(S["hot_ready"], 1)
                eng.wait_ge(S["listed"], 1)
                ch.add(eng.tensor_copy(c.slot_token[:, 0:NT], list_ps[:, 0:NT]))
                ch.settle()

            @block.tensor
            def _(eng):
                eng.sem_inc(S["placed"], TOPK - 1)
                eng.wait_ge(S["mask_ready"], 1)
                for t in range(TT):
                    eng.matmul(rank_ps[:, t * E:(t + 1) * E], c.tri[:], mask[:, t, :], start=True, stop=False)
                    eng.matmul(rank_ps[:, t * E:(t + 1) * E], c.ones[:], cum[:, t, :], start=False, stop=True)
                eng.matmul(count_ps[:, 0:E], c.ones[:], cum[:, TT, :], start=True, stop=True).then_inc(S["counted"], 1)

                def place(t, k, **flags):
                    eng.wait_ge(S["hot_ready"], (t * TOPK + (k + 1)) * 2)
                    return eng.matmul(list_ps[:, 0:NT], oh_lo[:, k], oh_hi[:, k], skip_group_check=True, **flags)\
                        .then_inc(S["placed"], 1)

                for k in range(TOPK):
                    place(0, k, start=(k == 0), stop=False)
                with eng.Fori(1, TT) as t:
                    for k in range(TOPK):
                        place(t, k, start=False, stop=False)
                eng.wait_ge(S["placed"], TT * TOPK + TOPK)
                eng.sem_inc(S["listed"], 1)


def experts(nc, c, dram):
    ctx = ExitStack()
    with ctx:
        def sb(name, shape, dt=F32):
            return ctx.enter_context(nc.sbuf_tensor(name, shape, dt))

        U = 4
        xT_ps = [ctx.enter_context(nc.psum_tensor(f"xT_ps{i}", [P, 512], F32)) for i in range(2)]
        h_ps = [ctx.enter_context(nc.psum_tensor(f"h_ps{i}", [P, 512], F32)) for i in range(2)]
        aT_ps = [ctx.enter_context(nc.psum_tensor(f"aT_ps{i}", [P, 512], F32)) for i in range(2)]
        y_ps = [ctx.enter_context(nc.psum_tensor(f"y_ps{i}", [P, 512], F32)) for i in range(2)]
        which = sb("which", [P, U], I32)
        xg = sb("xg", [P, U, DM])
        held = sb("held", [P, 1])
        xT = sb("xT", [P, 2, KC, P])
        gs = sb("gs", [P, 2, FI])
        act = sb("act", [P, 2, FI])
        aT = sb("aT", [P, 2, FC, P])
        y = sb("y", [P, U, DM])
        names = ("which_ready xT_done xT_ready h_done silu_done act_ready aT_done aT_ready y_done y_ready "
                 "expert_ready held").split()
        S = {n: ctx.enter_context(nc.semaphore("e_" + n)) for n in names}
        gathered = [ctx.enter_context(nc.semaphore(f"e_gathered{u}")) for u in range(U)]
        stored = [ctx.enter_context(nc.semaphore(f"e_stored{u}")) for u in range(U)]

        def tiles(eng, body):
            with eng.Fori(0, NT // U) as r:
                for p in range(0, U, 2):
                    body(r, p)

        with nc.Block() as block:
            @block.sync
            def _(eng):
                for e in range(RING - 1):
                    eng.wait_ge(c.w_landed[e], 32)
                    eng.sem_inc(S["expert_ready"], 1)
                with eng.Fori(0, E // RING - 1) as r:
                    for u in range(RING):
                        last = eng.value_load(c.expert_end[0:1, bass.ds(r * RING + u, 1)], min_val=1, max_val=NT + 1)
                        eng.wait_ge(S["y_done"], last)
                        ds = bass.ds(r * RING + (RING + u), 1)
                        eng.dma_start(c.w1r[:, u], dram.w1[ds].rearrange("a p k n -> (a p) k n")).then_inc(c.w_landed[u], 16)
                        eng.dma_start(c.w2r[:, u], dram.w2[ds].rearrange("a p k n -> (a p) k n")).then_inc(c.w_landed[u], 16)
                        prev = (u - 1) % RING
                        eng.wait_ge(c.w_landed[prev], r * 32 + (32 if u == 0 else 64))
                        eng.sem_inc(S["expert_ready"], 1)
                eng.wait_ge(c.w_landed[RING - 1], E // RING * 32)
                eng.sem_inc(S["expert_ready"], 1)

            @block.gpsimd
            def _(eng):
                eng.sem_inc(S["held"], 1)
                def gather(r, u):
                        eng.wait_ge(S["xT_done"], r * U + (u + 1))
                        eng.wait_ge(S["which_ready"], r * U + (u + 1))
                        eng.wait_ge(S["held"], r * U + (u + 1))
                        eng.tensor_tensor(held[:], c.ones[:, 0:1], c.ones[:, 0:1], ALU.mult).then_inc(S["held"], 1)
                        eng.indirect_dma_start(out=xg[:, u, :], out_offset=None, in_=dram.flat,
                                               in_offset=bass.IndirectOffsetOnAxis(ap=which[:, u:u + 1], axis=0))\
                            .then_inc(gathered[u], 16)

                with eng.Fori(0, NT // U) as r:
                    for u in range(U):
                        gather(r, u)
                for u in (0, 1):
                    gather(NT // U, u)

            @block.scalar
            def _(eng):
                for u in range(U):
                    eng.sem_inc(stored[u], 16)
                eng.sem_inc(S["aT_ready"], 2)

                def pair(r, p):
                    for i in (0, 1):
                        j = r * U + (p + i)
                        eng.wait_ge(S["h_done"], j + 1)
                        eng.wait_ge(S["act_ready"], j + 1)
                        eng.activation(gs[:, i], h_ps[i][:, 0:FI], ACT.Silu).then_inc(S["silu_done"], 1)
                    for i in (0, 1):
                        j = r * U + (p + i)
                        eng.wait_ge(S["aT_done"], j + (1 + 2))
                        eng.activation(aT[:, i], aT_ps[i][:, 0:FI].rearrange("p (k t) -> p k t", k=FC), ACT.Copy)\
                            .then_inc(S["aT_ready"], 1)
                    for i in (0, 1):
                        j = r * U + (p + i)
                        eng.wait_ge(S["y_ready"], j + (1 + 2))
                        eng.dma_start(dram.ys[bass.ds(j, 1)].rearrange("a p n -> (a p) n"), y[:, p + i, :])\
                            .then_inc(stored[p + i], 16)

                tiles(eng, pair)
                for u in range(U):
                    eng.wait_ge(stored[u], NT // U * 16 + 16)

            @block.vector
            def _(eng):
                eng.sem_inc(S["act_ready"], 2)
                eng.sem_inc(S["y_ready"], 2)
                eng.sem_inc(S["xT_ready"], 2)
                for u in range(U):
                    eng.tensor_copy(which[:, u:u + 1], c.slot_token[:, u:u + 1]).then_inc(S["which_ready"], 1)

                def rows_out(j, i):
                    eng.wait_ge(S["xT_done"], j + (1 + U))
                    eng.tensor_scalar(xT[:, i], xT_ps[i][:].rearrange("p (k t) -> p k t", k=KC), 0.0, None, ALU.add)\
                        .then_inc(S["xT_ready"], 1)

                def pair(r, p):
                    for i in (0, 1):
                        j = r * U + (p + i)
                        eng.wait_ge(S["silu_done"], j + 1)
                        eng.wait_ge(S["aT_done"], j + 1)
                        eng.tensor_tensor(act[:, i], gs[:, i], h_ps[i][:, FI:2 * FI], ALU.mult).then_inc(S["act_ready"], 1)
                    for i in (0, 1):
                        rows_out(r * U + (p + i + 2), i)
                    for i in (0, 1):
                        eng.wait_ge(gathered[p + i], r * 16 + 16)
                        eng.tensor_scalar(which[:, p + i:p + i + 1], c.slot_token[:, bass.ds(r * U + (p + i + U), 1)], 0.0, None,
                                          ALU.add).then_inc(S["which_ready"], 1)
                    for i in (0, 1):
                        j = r * U + (p + i)
                        eng.wait_ge(S["y_done"], j + 2)
                        eng.wait_ge(stored[p + i], r * 16 + 16)
                        eng.tensor_scalar(y[:, p + i, :], y_ps[i][:], 0.0, None, ALU.add).then_inc(S["y_ready"], 1)

                for i in (0, 1):
                    rows_out(i, i)
                tiles(eng, pair)

            @block.tensor
            def _(eng):
                eng.sem_inc(S["xT_done"], U)
                eng.sem_inc(S["aT_done"], 2)
                eng.sem_inc(S["y_done"], 1)

                def rows_in(j, p, i, pass_):
                    eng.wait_ge(gathered[p + i], pass_ * 16 + 16)
                    eng.wait_ge(S["xT_ready"], j + 1)
                    for k in range(KC):
                        ins = eng.transpose(xT_ps[i][:, k * P:(k + 1) * P], xg[:, p + i, k * P:(k + 1) * P], c.ident[:])
                    ins.then_inc(S["xT_done"], 1)

                def pair(r, p):
                    ring = []
                    for i in (0, 1):
                        j = r * U + (p + i)
                        ring.append(eng.value_load(c.tile_ring[0:1, bass.ds(j, 1)], min_val=0, max_val=RING - 1))
                        need = eng.value_load(c.tile_need[0:1, bass.ds(j, 1)], min_val=1, max_val=E)
                        eng.wait_ge(S["expert_ready"], need)
                        eng.wait_ge(S["xT_ready"], j + (1 + 2))
                        eng.wait_ge(S["act_ready"], j + 1)
                        for k in range(KC):
                            ins = eng.matmul(h_ps[i][:], xT[:, i, k, :], c.w1r[:, bass.ds(ring[i], 1), k, :].rearrange("p a n -> p (a n)"),
                                             start=(k == 0), stop=(k == KC - 1))
                        ins.then_inc(S["h_done"], 1)
                    for i in (0, 1):
                        rows_in(r * U + (p + i + 2), (p + 2) % U, i, r + (p + 2) // U)
                    for i in (0, 1):
                        j = r * U + (p + i)
                        eng.wait_ge(S["act_ready"], j + (1 + 2))
                        eng.wait_ge(S["aT_ready"], j + 1)
                        for k in range(FC):
                            ins = eng.transpose(aT_ps[i][:, k * P:(k + 1) * P], act[:, i, k * P:(k + 1) * P], c.ident[:])
                        ins.then_inc(S["aT_done"], 1)
                    for i in (0, 1):
                        j = r * U + (p + i)
                        eng.wait_ge(S["aT_ready"], j + (1 + 2))
                        eng.wait_ge(S["y_ready"], j + 1)
                        for k in range(FC):
                            ins = eng.matmul(y_ps[i][:], aT[:, i, k, :], c.w2r[:, bass.ds(ring[i], 1), k, :].rearrange("p a n -> p (a n)"),
                                             start=(k == 0), stop=(k == FC - 1))
                        ins.then_inc(S["y_done"], 1)

                for i in (0, 1):
                    rows_in(i, 0, i, 0)
                tiles(eng, pair)


def combine(nc, c, dram):
    ctx = ExitStack()
    with ctx:
        def sb(name, shape, dt=F32):
            return ctx.enter_context(nc.sbuf_tensor(name, shape, dt))

        U = 2
        where = sb("where", [P, U, TOPK], I32)
        rows = sb("rows", [P, U, TOPK, DM])
        held = sb("c_held", [P, 1])
        names = "where_ready added summed held".split()
        S = {n: ctx.enter_context(nc.semaphore("c_" + n)) for n in names}
        gathered = [ctx.enter_context(nc.semaphore(f"c_gathered{u}")) for u in range(U)]
        stored = ctx.enter_context(nc.semaphore("c_stored"))

        with nc.Block() as block:
            @block.gpsimd
            def _(eng):
                eng.sem_inc(S["held"], 1)
                with eng.Fori(0, TT // U) as r:
                    for u in range(U):
                        t = r * U + u
                        eng.wait_ge(S["summed"], t + 1)
                        eng.wait_ge(S["where_ready"], t + 1)
                        eng.wait_ge(S["held"], t + 1)
                        eng.tensor_tensor(held[:], c.ones[:, 0:1], c.ones[:, 0:1], ALU.mult).then_inc(S["held"], 1)
                        for k in range(TOPK):
                            eng.indirect_dma_start(out=rows[:, u, k, :], out_offset=None, in_=dram.ys_rows,
                                                   in_offset=bass.IndirectOffsetOnAxis(ap=where[:, u, k:k + 1], axis=0))\
                                .then_inc(gathered[u], 16)

            @block.vector
            def _(eng):
                eng.sem_inc(S["summed"], 2)
                for u in range(U):
                    eng.tensor_copy(where[:, u, :], c.dest[:, u, :]).then_inc(S["where_ready"], 1)
                with eng.Fori(0, TT // U) as r:
                    for u in range(U):
                        t = r * U + u
                        b = c.base[:, bass.ds(t, 1), :].rearrange("p a n -> p (a n)")
                        eng.wait_ge(gathered[u], r * (16 * TOPK) + 16 * TOPK)
                        eng.tensor_scalar(where[:, u, :], c.dest[:, bass.ds(t + U, 1), :].rearrange("p a k -> p (a k)"), 0.0,
                                          None, ALU.add).then_inc(S["where_ready"], 1)
                        for k in range(TOPK):
                            if k:
                                eng.wait_ge(S["added"], t * (TOPK - 1) + k)
                            w = c.weight[:, bass.ds(t, 1), k:k + 1].rearrange("p a k -> p (a k)")
                            eng.scalar_tensor_tensor(b, rows[:, u, k, :], w, b, ALU.mult, ALU.add)\
                                .then_inc(S["added" if k < TOPK - 1 else "summed"], 1)

            @block.sync
            def _(eng):
                with eng.Fori(0, TT) as t:
                    eng.wait_ge(S["summed"], t + (1 + 2))
                    eng.dma_start(dram.out[bass.ds(t, 1)].rearrange("a p n -> (a p) n"),
                                  c.base[:, bass.ds(t, 1), :].rearrange("p a n -> p (a n)")).then_inc(stored, 16)
                eng.wait_ge(stored, 16 * TT)


def build(nc, dram):
    class Shared:
        pass

    c = Shared()
    with ExitStack() as ctx:
        def sb(name, shape, dt=F32):
            return ctx.enter_context(nc.sbuf_tensor(name, shape, dt))

        constants(nc, c, ctx, dram)
        mamba(nc, c, dram)
        c.base = sb("base", [P, TT, DM])
        c.logits = sb("logits", [P, TT, E])
        c.weight = sb("weight", [P, TT, TOPK])
        c.dest = sb("dest", [P, TT + 2, TOPK])
        c.slot_token = sb("slot_token", [P, NT + RING])
        c.tile_ring, c.tile_need = sb("tile_ring", [1, NT], I32), sb("tile_need", [1, NT], I32)
        c.expert_end = sb("expert_end", [1, E], I32)
        c.w1r, c.w2r = sb("w1_ring", [P, RING, KC, 2 * FI]), sb("w2_ring", [P, RING, FC, DM])
        c.w_landed = [ctx.enter_context(nc.semaphore(f"w_landed{u}")) for u in range(RING)]
        c.flat_stored = ctx.enter_context(nc.semaphore("flat_stored"))
        tokens(nc, c, dram)
        routing(nc, c, dram)
        experts(nc, c, dram)
        combine(nc, c, dram)


class Dram:
    pass


def tensors(nc, arrays):
    def given(name):
        a = arrays[name]
        return nc.dram_tensor("in_" + name, a.shape, mybir.dt.from_np(a.dtype), kind="ExternalInput").ap()

    d = Dram()
    d.x, d.w_norm = given("x"), given("w_norm")
    d.w_in_x, d.w_in_res = given("w_in_x"), given("w_in_res")
    d.conv_w, d.conv_b = given("conv_w"), given("conv_b")
    d.b_dt, d.d_skip, d.a_log = given("b_dt"), given("d_skip"), given("a_log")
    d.w_xp, d.w_dt, d.w_out = given("w_xp"), given("w_dt"), given("w_out")
    d.norm_w, d.router_w = given("norm_w"), given("router_w")
    d.sg, d.su, d.sd = given("sg"), given("su"), given("sd")
    d.w1, d.w2 = given("w1"), given("w2")
    d.bcd = nc.dram_tensor("bcd", (NB * HALVES, 2 * NS, SEG), F32, kind="Internal").ap()
    d.out = nc.dram_tensor("out", (TT, P, DM), F32, kind="ExternalOutput").ap()
    d.x1 = nc.dram_tensor("x1", (TT, P, DM), F32, kind="Internal").ap()
    d.flat = nc.dram_tensor("flat", (T, DM), F32, kind="Internal").ap()
    d.flat_seg = d.flat.rearrange("(s t p) n -> s p t n", t=ST, p=P)
    d.ys = nc.dram_tensor("ys", (NT, P, DM), F32, kind="Internal").ap()
    d.ys_rows = d.ys.rearrange("j p n -> (j p) n")
    d.x_seg = d.x.rearrange("(s t) p n -> s p t n", t=ST)
    d.x1_seg = d.x1.rearrange("(s t) p n -> s p t n", t=ST)
    return d


def kernel(**inputs):
    import concourse.bacc as bacc
    from concourse.bass_utils import run_bass_kernel_spmd as run

    g = {k: np.asarray(v) for k, v in inputs.items()}
    a = lambda n: g["L0_attn_" + n]
    cont = np.ascontiguousarray
    col = lambda v, *rest: cont(np.moveaxis(v.reshape(-1, P, *rest), 0, 1))
    w_in = a("W_in").reshape(KC, P, 2, DC, P)
    arrays = {
        "x": cont(a("x").reshape(TT, P, DM)),
        "w_norm": cont(a("w_norm").reshape(1, DM)),
        "w_in_x": cont(w_in[:, :, 0].reshape(KC, P, DI).transpose(1, 0, 2)),
        "w_in_res": cont(w_in[:, :, 1].transpose(2, 1, 0, 3)),
        "conv_w": cont(a("conv_w").reshape(KW, DC, P).transpose(2, 1, 0)),
        "conv_b": col(a("conv_b")), "b_dt": col(a("b_dt")), "d_skip": col(a("D")),
        "a_log": cont(a("A_log").reshape(DC, P, NS).transpose(1, 0, 2).reshape(P, DC * NS)),
        "w_xp": col(a("W_xp"), DR + 2 * NS),
        "w_dt": cont(a("W_dt").reshape(DR, DC, P).transpose(1, 0, 2)),
        "w_out": col(a("W_out"), DM),
        "norm_w": cont(g["L0_ffn_norm_w"].reshape(1, DM)),
        "router_w": col(g["L0_ffn_router_w"].T, E),
        "sg": col(g["L0_ffn_sg"], SH), "su": col(g["L0_ffn_su"], SH), "sd": col(g["L0_ffn_sd"], DM),
        "w1": cont(g["L0_ffn_w1"].reshape(E, KC, P, 2 * FI).transpose(0, 2, 1, 3)),
        "w2": cont(g["L0_ffn_w2"].reshape(E, FC, P, DM).transpose(0, 2, 1, 3)),
    }
    nc = bacc.Bacc("TRN2", target_bir_lowering=False, num_devices=1)
    dram = tensors(nc, arrays)
    build(nc, dram)
    r = run(nc, [{"in_" + n: v for n, v in arrays.items()}], core_ids=[0])
    return r.results[0]["out"].reshape(NB, LEN, DM)
```

```python
from contextlib import ExitStack

import numpy as np

import concourse.bass as bass
from concourse import mybir

ALU = mybir.AluOpType
ACT = mybir.ActivationFunctionType
AX = mybir.AxisListType
F32 = mybir.dt.float32
F16 = mybir.dt.float16
I32 = mybir.dt.int32
U32 = mybir.dt.uint32

P = 128
NB, LEN, DM = 2, 1024, 512
T = NB * LEN
TT = T // P
DI, NS, DR, KW = 1024, 16, 128, 4
KC = DM // P
DC = DI // P
SEG = 512
HALVES = LEN // SEG
ST = SEG // P
Q = 4
NQ = NS // Q
E, FI, TOPK = 32, 256, 4
FC = FI // P
SH = 512
NT = T * TOPK // P + E
RING = 4
PASS = 4
COMBINED = 4
EPS_LN, EPS_RMS_A, EPS_RMS_F = 1e-5, 1e-5, 1e-6
EXP_TABLES = "exp_and_others"


class Chain:

    def __init__(self, eng, sem, base=0):
        self.eng, self.sem, self.base, self.n = eng, sem, base, 0

    def add(self, ins):
        ins.then_inc(self.sem, 1)
        self.n += 1

    def settle(self):
        self.eng.wait_ge(self.sem, self.base + self.n)


def bcast(ap, shape):
    return ap.to_broadcast(shape)


def constants(nc, c, ctx, dram):
    sb = lambda name, shape, dt=F32: ctx.enter_context(nc.sbuf_tensor(name, shape, dt))
    c.ident, c.ones, c.tri = sb("ident", [P, P]), sb("ones", [P, P]), sb("tri", [P, P])
    made = ctx.enter_context(nc.semaphore("const_made"))
    with nc.Block() as block:
        @block.gpsimd
        def _(eng):
            eng.memset(c.ident[:], 0.0).then_inc(made, 1)
            eng.memset(c.ones[:], 1.0).then_inc(made, 1)
            eng.wait_ge(made, 2)
            eng.affine_select(out=c.ident[:], in_=c.ident[:], compare_op=ALU.not_equal, fill=1.0, base=0,
                              pattern=[[-1, P]], channel_multiplier=1).then_inc(made, 1)
            eng.affine_select(out=c.tri[:], in_=c.ones[:], compare_op=ALU.is_gt, fill=0.0, base=0,
                              pattern=[[1, P]], channel_multiplier=-1).then_inc(made, 1)
            eng.wait_ge(made, 4)


def mamba(nc, c, dram):
    ctx = ExitStack()
    with ctx:
        def sb(name, shape, dt=F32):
            return ctx.enter_context(nc.sbuf_tensor(name, shape, dt))

        def sem(name):
            return ctx.enter_context(nc.semaphore(name))

        bank = [ctx.enter_context(nc.psum_tensor(f"bank{i}", [P, SEG], F32)) for i in range(8)]
        w_in = sb("w_in", [P, KC, DI])
        w_xp = sb("w_xp", [P, DC, DR + 2 * NS])
        w_out = sb("w_out", [P, DC, DM])
        conv_w, conv_b = sb("conv_w_sb", [P, DC, KW]), sb("conv_b_sb", [P, DC])
        b_dt, d_skip = sb("b_dt_sb", [P, DC]), sb("d_skip", [P, DC])
        a_neg = sb("a_neg", [P, DC * NS])
        norm_w = sb("norm_w_a", [P, DM])
        w_res = sb("w_res", [P, 2, KC, P])
        w_dt = sb("w_dt_sb", [P, 2, P])
        b_rep, c_rep = sb("b_rep", [P, NS, SEG]), sb("c_rep", [P, NS, SEG])
        xin = sb("xin", [P, 2, ST, DM])
        xnT = sb("xnT", [P, KC, SEG])
        xraw = sb("xraw", [P, 2, KW - 1 + SEG])
        hist = sb("hist", [P, DC, KW - 1])
        xs = sb("xs", [P, DC, SEG])
        dtr = sb("dtr", [P, SEG])
        bc = sb("bc", [2 * NS, SEG])
        delta = sb("delta", [P, 2, SEG])
        spl = xraw[:, :, 0:SEG]
        zs = sb("zs", [P, 2, SEG])
        xd = sb("xd", [P, SEG])
        cv = zs
        h = sb("h", [P, NQ, Q, SEG])
        state = sb("state", [P, DC * NS])
        st6, mv = sb("st6", [P, ST, 6]), sb("mv", [P, ST, 2])
        var1, rstd = sb("var1", [P, ST]), sb("rstd", [P, ST])
        ssq, ms, rrms = sb("ssq", [P, ST]), sb("ms", [P, ST]), sb("rrms", [P, ST])
        xl = h[:, 0, :, :]
        junk = h[:, 1, :, :]

        names = ("w_loaded small_loaded aneg_ready x_loaded var_ready rstd_ready xl_ready ssq_ready xr_ready ms_ready rrms_ready "
                 "xn_ready tp_done tp_evac in_done in_evac conv_done xs_ready bc_done xp_done dtr_ready bc_ready "
                 "bcd_written dtp_done resp_done a_evac sp_ready delta_ready du_ready z_evac da_ready "
                 "scan_done state_saved bquad_used cmul_done y_summed xd_ready yg_ready op_done x1_ready x1_stored "
                 "norm_chain conv_chain act_chain sp_chain").split()
        S = {n: sem("m_" + n) for n in names}
        b_loaded = [sem(f"m_b_loaded{q}") for q in range(NQ)]
        c_loaded = [sem(f"m_c_loaded{q}") for q in range(NQ)]
        wslot = [sem(f"m_wslot{u}") for u in range(2)]

        small = [(norm_w[:], bcast(dram.w_norm, [P, DM])), (a_neg[:], dram.a_log), (conv_w[:], dram.conv_w),
                 (conv_b[:], dram.conv_b), (b_dt[:], dram.b_dt), (d_skip[:], dram.d_skip)]
        loads = [(w_in[:], dram.w_in_x), (w_xp[:], dram.w_xp), (w_out[:], dram.w_out)]
        NSM, NW = 16 * len(small), 16 * len(loads)
        NORM_LINKS, CONV_LINKS, ACT_LINKS = 2 * ST + 1, DC * (KW + 1), 2

        def segments(eng, norm, body, after=lambda s, th: None):
            norm(0, 0)
            with eng.Fori(0, NB) as b:
                for th in range(HALVES):
                    s = b * HALVES + th
                    body(b, th, s)
                    norm(s + 1, 1 - th)
                    after(s, th)

        def chunks(eng, body):
            body(0, 0, True, False)
            with eng.Fori(0, (DC - 2) // 2) as r:
                for k in range(2):
                    body(r * 2 + (1 + k), (1 + k) % 2, False, False)
            body(DC - 1, (DC - 1) % 2, False, True)

        with nc.Block() as block:
            @block.sync
            def _(eng):
                eng.sem_inc(S["x1_stored"], 16)
                eng.dma_start(xin[:, 0], dram.x_seg[0]).then_inc(S["x_loaded"], 16)
                for dst, src in small:
                    eng.dma_start(dst, src).then_inc(S["small_loaded"], 16)
                for dst, src in loads:
                    eng.dma_start(dst, src).then_inc(S["w_loaded"], 16)

                def load_x(s, half):
                    eng.dma_start(xin[:, half], dram.x_seg[bass.ds(s, 1)].rearrange("a p t n -> (a p) t n"))\
                        .then_inc(S["x_loaded"], 16)

                def segment(b, th, s):
                    def slot(d, u):
                        g = s * DC + d
                        eng.wait_ge(S["resp_done"], g + 1)
                        dd = bass.ds(d, 1)
                        eng.dma_start(w_res[:, u], dram.w_in_res[dd].rearrange("a p k n -> (a p) k n"))\
                            .then_inc(wslot[u], 16)
                        eng.dma_start(w_dt[:, u], dram.w_dt[dd].rearrange("a p n -> (a p) n")).then_inc(wslot[u], 16)

                    slot(0, 0)
                    slot(1, 1)
                    eng.wait_ge(S["bc_ready"], s + 1)
                    eng.dma_start(dram.bcd[bass.ds(s, 1)].rearrange("a n t -> (a n) t"), bc[:])\
                        .then_inc(S["bcd_written"], 16)
                    eng.wait_ge(S["bcd_written"], (s + 1) * 16)
                    for q in range(NQ):
                        for (dst, loaded, used, off) in ((b_rep, b_loaded, "bquad_used", 0), (c_rep, c_loaded, "cmul_done", NS)):
                            eng.wait_ge(S[used], s * (DC * NQ) - (NQ - 1 - q) + DC * NQ)
                            src = dram.bcd[bass.ds(s, 1), off + Q * q:off + Q * q + Q, :]
                            eng.dma_start(dst[:, Q * q:Q * q + Q, :], src.to_broadcast([P, Q, SEG]))\
                                .then_inc(loaded[q], 16)
                    eng.wait_ge(S["x1_stored"], s * (16 * ST) + 16)
                    load_x(b * HALVES + 1 if th == 0 else (b * -1 + 1) * HALVES, 1 - th)
                    with eng.Fori(0, (DC - 2) // 2) as r:
                        for k in range(2):
                            slot(r * 2 + (2 + k), k)
                    for i in range(ST):
                        eng.wait_ge(S["x1_ready"], s * ST + (i + 1))
                        eng.dma_start(dram.x1_seg[bass.ds(s, 1), :, i, :].rearrange("a p n -> (a p) n"), xin[:, th, i, :])\
                            .then_inc(S["x1_stored"], 16)

                segments(eng, lambda s, half: None, segment)
                eng.wait_ge(S["x1_stored"], 16 * TT + 16)

            @block.scalar
            def _(eng):
                eng.sem_inc(S["in_evac"], 2)
                eng.sem_inc(S["tp_evac"], 2)
                eng.sem_inc(S["a_evac"], 1)
                eng.sem_inc(S["z_evac"], 1)
                eng.sem_inc(S["xs_ready"], 2)
                eng.wait_ge(S["small_loaded"], NSM)
                eng.activation(a_neg[:], a_neg[:], ACT.Exp).then_inc(S["aneg_ready"], 1)
                eng.wait_ge(S["aneg_ready"], 2)

                def norm(s, half):
                    ch = Chain(eng, S["act_chain"], s * ACT_LINKS)
                    eng.wait_ge(S["var_ready"], s + 1)
                    ch.add(eng.activation(rstd[:], var1[:], ACT.Ln))
                    ch.settle()
                    eng.activation(rstd[:], rstd[:], ACT.Exp, scale=-0.5).then_inc(S["rstd_ready"], 1)
                    for i in range(ST):
                        eng.wait_ge(S["xl_ready"], s * ST + (i + 1))
                        eng.activation(junk[:, i, :], xl[:, i, :], ACT.Square, accum_out=ssq[:, i:i + 1])\
                            .then_inc(S["ssq_ready"], 1)
                    eng.wait_ge(S["ms_ready"], s + 1)
                    ch.add(eng.activation(rrms[:], ms[:], ACT.Ln))
                    ch.settle()
                    eng.activation(rrms[:], rrms[:], ACT.Exp, scale=-0.5).then_inc(S["rrms_ready"], 1)
                    for i in range(ST):
                        eng.wait_ge(S["tp_done"], s * ST + (i + 1))
                        eng.activation(xnT[:, :, i * P:(i + 1) * P],
                                       bank[6 + i % 2][:].rearrange("p (k t) -> p k t", k=KC), ACT.Copy)\
                            .then_inc(S["tp_evac"], 1)
                    assert ch.n == ACT_LINKS, ch.n

                def segment(b, th, s):
                    def silu(d):
                        eng.wait_ge(S["conv_done"], s * DC + (d + 1 + 2))
                        eng.activation(xs[:, d, :], cv[:, d % 2, :], ACT.Silu).then_inc(S["xs_ready"], 1)

                    for d in range(DC):
                        eng.wait_ge(S["in_done"], s * DC + (d + 1))
                        eng.wait_ge(S["conv_done"], s * DC + (d + 1))
                        eng.activation(xraw[:, d % 2, KW - 1:], bank[4 + d % 2][:], ACT.Copy).then_inc(S["in_evac"], 1)
                        if d:
                            silu(d - 1)
                    silu(DC - 1)
                    eng.preload_act_table_set(EXP_TABLES)
                    eng.wait_ge(S["xp_done"], s + 1)
                    eng.activation(dtr[:], bank[6][:], ACT.Copy).then_inc(S["dtr_ready"], 1)

                    def prep_a(d, u):
                        g = s * DC + d
                        eng.wait_ge(S["dtp_done"], g + 1)
                        eng.wait_ge(S["du_ready"], g + 1)
                        eng.activation(spl[:, u, :], bank[7][:], ACT.Abs, bias=b_dt[:, bass.ds(d, 1)])\
                            .then_inc(S["sp_chain"], 1)
                        eng.activation(delta[:, u, :], bank[7][:], ACT.Identity, bias=b_dt[:, bass.ds(d, 1)])\
                            .then_inc(S["a_evac"], 1)
                        eng.wait_ge(S["sp_chain"], g * 2 + 1)
                        eng.activation(spl[:, u, :], spl[:, u, :], ACT.Exp, scale=-1.0).then_inc(S["sp_chain"], 1)

                    def prep_b(d, u):
                        g = s * DC + d
                        eng.wait_ge(S["sp_chain"], g * 2 + 2)
                        eng.activation(spl[:, u, :], spl[:, u, :], ACT.Ln, bias=c.ones[:, 0:1])\
                            .then_inc(S["sp_ready"], 1)

                    def prep_c(d, u):
                        g = s * DC + d
                        eng.wait_ge(S["resp_done"], g + 1 + 2)
                        eng.wait_ge(S["yg_ready"], g + 1)
                        eng.activation(zs[:, u, :], bank[7][:], ACT.Silu).then_inc(S["z_evac"], 1)

                    prep_a(0, 0)
                    prep_b(0, 0)

                    def chunk(d, u, first, last):
                        g = s * DC + d
                        eng.wait_ge(S["delta_ready"], g + 1)
                        for q in range(NQ):
                            for j in range(Q):
                                eng.wait_ge(S["scan_done"], g * NS + (q * Q + j + 1))
                                eng.activation(bank[j][:], delta[:, u, :], ACT.Exp,
                                               scale=a_neg[:, bass.ds(d * NS + (q * Q + j), 1)]).then_inc(S["da_ready"], 1)
                            if q == 0:
                                eng.wait_ge(S["y_summed"], g * NQ + 1)
                                eng.activation(xd[:], xs[:, bass.ds(d, 1), :].rearrange("p a t -> p (a t)"), ACT.Copy,
                                               scale=d_skip[:, bass.ds(d, 1)]).then_inc(S["xd_ready"], 1)
                            if first and q == 0:
                                prep_c(d, u)
                            if not last and q == 1:
                                prep_a(d + 1, 1 - u)
                            if not last and q == 2:
                                prep_b(d + 1, 1 - u)
                            if not last and q == 3:
                                prep_c(d + 1, 1 - u)

                    chunks(eng, chunk)

                segments(eng, norm, segment)

            @block.vector
            def _(eng):
                eng.sem_inc(S["scan_done"], Q)
                eng.sem_inc(S["bquad_used"], DC * NQ)
                eng.sem_inc(S["du_ready"], 2)
                eng.sem_inc(S["yg_ready"], 2)
                eng.sem_inc(S["conv_done"], 2)
                eng.wait_ge(S["small_loaded"], NSM)
                eng.wait_ge(S["aneg_ready"], 1)
                eng.tensor_scalar(a_neg[:], a_neg[:], -1.0, None, ALU.mult).then_inc(S["aneg_ready"], 1)

                def norm(s, half):
                    ch = Chain(eng, S["norm_chain"], s * NORM_LINKS)
                    eng.wait_ge(S["x_loaded"], (s + 1) * 16)
                    for i in range(ST):
                        ch.add(eng.bn_stats(st6[:, i, :], xin[:, half, i, :]))
                    ch.settle()
                    ch.add(eng.memset(var1[:], 0.0))
                    for i in range(ST):
                        ch.add(eng.bn_aggr(mv[:, i, :], st6[:, i, :]))
                    ch.settle()
                    eng.tensor_scalar(var1[:], mv[:, :, 1], EPS_LN, None, ALU.add).then_inc(S["var_ready"], 1)
                    eng.wait_ge(S["rstd_ready"], s + 1)
                    for i in range(ST):
                        eng.tensor_scalar(xl[:, i, :], xin[:, half, i, :], mv[:, i, 0:1], rstd[:, i:i + 1],
                                          ALU.subtract, ALU.mult).then_inc(S["xl_ready"], 1)
                    eng.wait_ge(S["ssq_ready"], (s + 1) * ST)
                    eng.tensor_scalar(ms[:], ssq[:], 1.0 / DM, EPS_RMS_A, ALU.mult, ALU.add).then_inc(S["ms_ready"], 1)
                    eng.wait_ge(S["rrms_ready"], s + 1)
                    eng.wait_ge(S["xr_ready"], (s + 1) * ST)
                    for i in range(ST):
                        eng.scalar_tensor_tensor(xl[:, i, :], xl[:, i, :], rrms[:, i:i + 1], norm_w[:],
                                                 ALU.mult, ALU.mult).then_inc(S["xn_ready"], 1)
                    assert ch.n == NORM_LINKS, ch.n

                def segment(b, th, s):
                    ch = Chain(eng, S["conv_chain"], s * CONV_LINKS)
                    for d in range(DC):
                        x = xraw[:, d % 2, :]
                        if th == 0:
                            ch.add(eng.memset(x[:, 0:KW - 1], 0.0))
                        else:
                            ch.add(eng.tensor_copy(x[:, 0:KW - 1], hist[:, d, :]))
                        eng.wait_ge(S["in_evac"], s * DC + (d + 1 + 2))
                        eng.wait_ge(S["xs_ready"], s * DC + (d + 1))
                        ch.settle()
                        y = cv[:, d % 2, :]
                        ch.add(eng.tensor_scalar(y, x[:, KW - 1:], conv_w[:, d, KW - 1:KW], conv_b[:, d:d + 1],
                                                 ALU.mult, ALU.add))
                        for k in range(KW - 2, -1, -1):
                            ch.settle()
                            ch.add(eng.scalar_tensor_tensor(y, x[:, k:k + SEG], conv_w[:, d, k:k + 1], y, ALU.mult, ALU.add))
                        eng.tensor_copy(hist[:, d, :], x[:, SEG:SEG + KW - 1]).then_inc(S["conv_done"], 1)

                    eng.wait_ge(S["bc_done"], s + 1)
                    eng.tensor_copy(bc[:], bank[7][0:2 * NS, :]).then_inc(S["bc_ready"], 1)

                    def softplus(d, u):
                        g = s * DC + d
                        eng.wait_ge(S["sp_ready"], g + 1)
                        eng.scalar_tensor_tensor(delta[:, u, :], delta[:, u, :], 0.0, spl[:, u, :], ALU.max, ALU.add)\
                            .then_inc(S["delta_ready"], 1)

                    def delta_x(d, u):
                        g = s * DC + d
                        eng.wait_ge(S["delta_ready"], g + 1)
                        eng.wait_ge(S["bquad_used"], g * NQ + DC * NQ)
                        eng.tensor_tensor(bank[6][:], delta[:, u, :], xs[:, bass.ds(d, 1), :].rearrange("p a t -> p (a t)"),
                                          ALU.mult).then_inc(S["du_ready"], 1)

                    def gating(d, u):
                        g = s * DC + d
                        x = xs[:, bass.ds(d, 1), :].rearrange("p a t -> p (a t)")
                        eng.wait_ge(S["y_summed"], g * NQ + (NQ + NQ))
                        eng.wait_ge(S["z_evac"], g + 1 + 1)
                        eng.tensor_tensor(x, bank[4 + u][:], zs[:, u, :], ALU.mult).then_inc(S["yg_ready"], 1)

                    def spread(d, q, first):
                        g = s * DC + d
                        if first:
                            eng.wait_ge(b_loaded[q], (s + 1) * 16)
                        if q == 0:
                            eng.wait_ge(S["du_ready"], g + (1 + 2))
                        eng.wait_ge(S["y_summed"], g * NQ + (q + 1))
                        eng.tensor_tensor(h[:, q], bank[6][:].unsqueeze(1).to_broadcast([P, Q, SEG]),
                                          b_rep[:, Q * q:Q * q + Q, :], ALU.mult).then_inc(S["bquad_used"], 1)

                    softplus(0, 0)
                    delta_x(0, 0)
                    spread(0, 0, True)

                    def chunk(d, u, first, last):
                        g = s * DC + d
                        for q in range(NQ):
                            G = g * NQ + q
                            if q < NQ - 1:
                                spread(d, q + 1, first)
                            eng.wait_ge(S["bquad_used"], G + (1 + DC * NQ))
                            for j in range(Q):
                                eng.wait_ge(S["da_ready"], g * NS + (q * Q + j + 1))
                                init = 0.0 if th == 0 else state[:, bass.ds(d * NS + (q * Q + j), 1)]
                                eng.tensor_tensor_scan(h[:, q, j, :], bank[j][:], h[:, q, j, :], init,
                                                       ALU.mult, ALU.add).then_inc(S["scan_done"], 1)
                                if not last and q == NQ - 1 and j == 0:
                                    delta_x(d + 1, 1 - u)
                            if not first and q == 1:
                                gating(d - 1, 1 - u)
                            if not last and q == NQ - 2:
                                softplus(d + 1, 1 - u)
                        if not last:
                            spread(d + 1, 0, False)

                    chunks(eng, chunk)
                    gating(DC - 1, (DC - 1) % 2)
                    assert ch.n == CONV_LINKS, ch.n

                def residual(s, th):
                    for i in range(ST):
                        eng.wait_ge(S["op_done"], s * ST + (i + 1))
                        eng.tensor_tensor(xin[:, th, i, :], xin[:, th, i, :], bank[i][:], ALU.add)\
                            .then_inc(S["x1_ready"], 1)

                segments(eng, norm, segment, residual)

            @block.gpsimd
            def _(eng):
                eng.sem_inc(S["cmul_done"], DC * NQ)

                def norm(s, half):
                    for i in range(ST):
                        eng.wait_ge(S["xl_ready"], s * ST + (i + 1))
                        x = xin[:, half, i, :]
                        eng.tensor_tensor(x, x, xl[:, i, :], ALU.add).then_inc(S["xr_ready"], 1)

                def segment(b, th, s):
                    def chunk(d, u, first, last):
                        g = s * DC + d
                        for q in range(NQ):
                            G = g * NQ + q
                            if first:
                                eng.wait_ge(c_loaded[q], (s + 1) * 16)
                            eng.wait_ge(S["scan_done"], g * NS + (q * Q + Q + Q))
                            if th == 0:
                                eng.tensor_tensor(state[:, bass.ds(d * NS + q * Q, Q)], h[:, q, :, SEG - 1], c.ones[:, 0:Q],
                                                  ALU.mult).then_inc(S["state_saved"], 1)
                                eng.wait_ge(S["state_saved"], b * (DC * NQ) + d * NQ + (q + 1))
                            eng.tensor_tensor(h[:, q], h[:, q], c_rep[:, Q * q:Q * q + Q, :], ALU.mult)\
                                .then_inc(S["cmul_done"], 1)

                    chunks(eng, chunk)

                segments(eng, norm, segment)

            @block.tensor
            def _(eng):
                eng.sem_inc(S["resp_done"], 2)
                eng.sem_inc(S["y_summed"], NQ)
                eng.wait_ge(S["w_loaded"], NW)

                def transposes(s, i):
                    eng.wait_ge(S["xn_ready"], s * ST + (i + 1))
                    eng.wait_ge(S["tp_evac"], s * ST + (i + 1))
                    for k in range(KC):
                        ins = eng.transpose(bank[6 + i % 2][:, k * P:(k + 1) * P], xl[:, i, k * P:(k + 1) * P], c.ident[:])
                    ins.then_inc(S["tp_done"], 1)

                def segment(b, th, s):
                    eng.wait_ge(S["tp_evac"], s * ST + (ST + 2))
                    for d in range(DC):
                        eng.wait_ge(S["in_evac"], s * DC + (d + 1))
                        for k in range(KC):
                            ins = eng.matmul(bank[4 + d % 2][:], w_in[:, k, d * P:(d + 1) * P], xnT[:, k, :],
                                             start=(k == 0), stop=(k == KC - 1))
                        ins.then_inc(S["in_done"], 1)
                    for d in range(DC):
                        eng.wait_ge(S["xs_ready"], s * DC + (d + 1 + 2))
                        ins = eng.matmul(bank[7][0:2 * NS, :], w_xp[:, d, DR:], xs[:, d, :], start=(d == 0), stop=(d == DC - 1))
                    ins.then_inc(S["bc_done"], 1)
                    for d in range(DC):
                        ins = eng.matmul(bank[6][:], w_xp[:, d, 0:DR], xs[:, d, :], start=(d == 0), stop=(d == DC - 1))
                    ins.then_inc(S["xp_done"], 1)
                    eng.wait_ge(S["dtr_ready"], s + 1)
                    eng.wait_ge(S["bc_ready"], s + 1)
                    eng.wait_ge(S["in_evac"], s * DC + (DC + 2))

                    def prep(d, u, uses):
                        g = s * DC + d
                        eng.wait_ge(wslot[u], (s * (DC // 2) + uses) * 32)
                        eng.wait_ge(S["z_evac"], g + 1)
                        eng.matmul(bank[7][:], w_dt[:, u, :], dtr[:], start=True, stop=True).then_inc(S["dtp_done"], 1)
                        eng.wait_ge(S["a_evac"], g + 1 + 1)
                        for k in range(KC):
                            ins = eng.matmul(bank[7][:], w_res[:, u, k, :], xnT[:, k, :], start=(k == 0), stop=(k == KC - 1))
                        ins.then_inc(S["resp_done"], 1)

                    prep(0, 0, 1)

                    def chunk(d, u, first, last):
                        g = s * DC + d
                        if not last:
                            prep(d + 1, 1 - u, 1 if first else pos["r"] + 2)
                        eng.wait_ge(S["yg_ready"], g + 1)
                        for q in range(NQ):
                            G = g * NQ + q
                            if q == 0:
                                eng.wait_ge(S["xd_ready"], g + 1)
                                eng.matmul(bank[4 + u][:], c.ident[:], xd[:], start=True, stop=False)
                            eng.wait_ge(S["cmul_done"], G + (1 + DC * NQ))
                            for j in range(Q):
                                ins = eng.matmul(bank[4 + u][:], c.ident[:], h[:, q, j, :],
                                                 start=False, stop=(q == NQ - 1 and j == Q - 1))
                            ins.then_inc(S["y_summed"], 1)

                    pos = {}

                    chunk(0, 0, True, False)
                    with eng.Fori(0, (DC - 2) // 2) as r:
                        pos["r"] = r
                        for k in range(2):
                            chunk(r * 2 + (1 + k), (1 + k) % 2, False, False)
                    chunk(DC - 1, (DC - 1) % 2, False, True)

                    eng.wait_ge(S["yg_ready"], s * DC + (DC + 1))
                    eng.wait_ge(S["z_evac"], s * DC + (DC + 1))
                    eng.wait_ge(S["scan_done"], (s + 1) * (DC * NS) + Q)
                    for i in range(ST):
                        for d in range(DC - 1):
                            eng.matmul(bank[i][:], xs[:, d, i * P:(i + 1) * P], w_out[:, d, :], start=(d == 0), stop=False)
                    eng.wait_ge(S["yg_ready"], s * DC + (DC + 2))
                    for i in range(ST):
                        transposes(s + 1, i)
                        eng.matmul(bank[i][:], xs[:, DC - 1, i * P:(i + 1) * P], w_out[:, DC - 1, :], start=False, stop=True)\
                            .then_inc(S["op_done"], 1)

                for i in range(ST):
                    transposes(0, i)
                segments(eng, lambda s, half: None, segment)


def tokens(nc, c, dram):
    ctx = ExitStack()
    with ctx:
        def sb(name, shape, dt=F32):
            return ctx.enter_context(nc.sbuf_tensor(name, shape, dt))

        bank = [ctx.enter_context(nc.psum_tensor(f"tbank{i}", [P, 512], F32)) for i in range(8)]
        norm_w = sb("norm_w_f", [P, DM])
        w_r = sb("w_router", [P, KC, E])
        w_g, w_u, w_d = sb("w_sg", [P, KC, SH]), sb("w_su", [P, KC, SH]), sb("w_sd", [P, SH // P, DM])
        x1 = sb("x1_group", [P, ST, DM])
        xl = sb("xl_group", [P, ST, DM])
        flat = sb("flat_group", [P, ST, DM])
        junk = sb("square_group", [P, ST, DM])
        flT = sb("flat_T", [P, ST, KC, P])
        gs = sb("gate_silu", [P, 2, SH])
        act = sb("act_shared", [P, 2, SH])
        actT = sb("act_shared_T", [P, 2, SH // P, P])
        st6, mv = sb("f_st6", [P, ST, 6]), sb("f_mv", [P, ST, 2])
        var1, rstd = sb("f_var", [P, ST]), sb("f_rstd", [P, ST])
        ssq, ms, rrms = sb("f_ssq", [P, ST]), sb("f_ms", [P, ST]), sb("f_rrms", [P, ST])
        names = ("norm_w_loaded w_loaded filled x_loaded var_ready rstd_ready xl_ready ssq_ready base_ready "
                 "ms_ready rrms_ready flat_ready "
                 "tp_done tp_evac gu_done silu_done act_ready at_done at_evac sd_done sd_added logits_done "
                 "logits_read dve_chain act_chain").split()
        S = {n: ctx.enter_context(nc.semaphore("t_" + n)) for n in names}
        loads = [(w_r[:], dram.router_w), (w_g[:], dram.sg),
                 (w_u[:], dram.su), (w_d[:], dram.sd)]
        NG = TT // ST
        DVE_LINKS = 2 * ST + 1

        def interleaved(eng, norm_steps, work_steps, order):
            for step in norm_steps(0):
                step()
            with eng.Fori(0, NG - 1) as r:
                n, w = iter(norm_steps(r + 1)), iter(work_steps(r))
                for kind in order:
                    next(n if kind == "n" else w)()
            for step in work_steps(NG - 1):
                step()

        with nc.Block() as block:
            @block.sync
            def _(eng):
                eng.dma_start(norm_w[:], bcast(dram.norm_w, [P, DM])).then_inc(S["norm_w_loaded"], 16)

                def load(g):
                    eng.dma_start(x1[:], dram.x1_seg[bass.ds(g, 1)].rearrange("a p t n -> (a p) t n"))\
                        .then_inc(S["x_loaded"], 16)

                def fill(g):
                    src = norm_w[:].unsqueeze(1).to_broadcast([P, E // NG, DM])
                    eng.dma_start(dram.ys[bass.ds(g * (E // NG) + (NT - E), E // NG)].rearrange("a p n -> p a n"), src)\
                        .then_inc(S["filled"], 16)

                def store(g):
                    eng.wait_ge(S["flat_ready"], g * ST + ST)
                    eng.dma_start(dram.flat_seg[bass.ds(g, 1)].rearrange("a p t n -> (a p) t n"), flat[:])\
                        .then_inc(c.flat_stored, 16)

                load(0)
                for dst, src in loads:
                    eng.dma_start(dst, src).then_inc(S["w_loaded"], 16)
                eng.wait_ge(S["norm_w_loaded"], 16)
                for e in range(RING):
                    eng.dma_start(c.w1r[:, e], dram.w1[e]).then_inc(c.w_landed[e], 16)
                    eng.dma_start(c.w2r[:, e], dram.w2[e]).then_inc(c.w_landed[e], 16)
                with eng.Fori(0, NG - 1) as r:
                    eng.wait_ge(S["base_ready"], r * ST + ST)
                    eng.wait_ge(S["xl_ready"], r * ST + ST)
                    load(r + 1)
                    store(r)
                    fill(r)
                store(NG - 1)
                fill(NG - 1)
                eng.wait_ge(S["filled"], 16 * NG)
                eng.wait_ge(c.flat_stored, 16 * NG)

            @block.scalar
            def _(eng):
                eng.sem_inc(S["tp_evac"], 2)
                eng.sem_inc(S["at_evac"], 1)

                def norm_steps(g):
                    ch = Chain(eng, S["act_chain"], g * 2)

                    def layer_rstd():
                        eng.wait_ge(S["var_ready"], g + 1)
                        ch.add(eng.activation(rstd[:], var1[:], ACT.Ln))
                        ch.settle()
                        eng.activation(rstd[:], rstd[:], ACT.Exp, scale=-0.5).then_inc(S["rstd_ready"], 1)

                    def squares():
                        for i in range(ST):
                            eng.wait_ge(S["xl_ready"], g * ST + (i + 1))
                            eng.activation(junk[:, i, :], xl[:, i, :], ACT.Square, accum_out=ssq[:, i:i + 1])\
                                .then_inc(S["ssq_ready"], 1)

                    def rms_rstd():
                        eng.wait_ge(S["ms_ready"], g + 1)
                        ch.add(eng.activation(rrms[:], ms[:], ACT.Ln))
                        ch.settle()
                        eng.activation(rrms[:], rrms[:], ACT.Exp, scale=-0.5).then_inc(S["rrms_ready"], 1)

                    return layer_rstd, squares, rms_rstd

                def work_steps(g):
                    def transposed(i):
                        eng.wait_ge(S["tp_done"], g * ST + (i + 1))
                        eng.activation(flT[:, i], bank[i % 2][:].rearrange("p (k t) -> p k t", k=KC), ACT.Copy)\
                            .then_inc(S["tp_evac"], 1)

                    def silu(i):
                        eng.wait_ge(S["gu_done"], g * ST + (i + 1))
                        eng.wait_ge(S["act_ready"], g * ST + (i + 1))
                        eng.activation(gs[:, i % 2], bank[3 + 2 * (i % 2)][:], ACT.Silu).then_inc(S["silu_done"], 1)

                    def act_transposed(i):
                        eng.wait_ge(S["at_done"], g * ST + (i + 1 + 2))
                        eng.wait_ge(S["sd_done"], g * ST + (i + 1))
                        eng.activation(actT[:, i % 2], bank[7][:].rearrange("p (k t) -> p k t", k=SH // P), ACT.Copy)\
                            .then_inc(S["at_evac"], 1)

                    return [lambda f=f, i=i: f(i) for f, i in (
                        (transposed, 0), (transposed, 1), (silu, 0), (transposed, 2), (transposed, 3),
                        (act_transposed, 0), (silu, 1), (act_transposed, 1), (silu, 2), (act_transposed, 2), (silu, 3),
                        (act_transposed, 3))]

                interleaved(eng, norm_steps, work_steps, "wwwwwwwnwwnnwww")

            @block.vector
            def _(eng):
                eng.sem_inc(S["act_ready"], 2)
                eng.sem_inc(S["sd_added"], 2)
                eng.sem_inc(S["logits_read"], 1)
                eng.wait_ge(S["norm_w_loaded"], 16)

                def norm_steps(g):
                    ch = Chain(eng, S["dve_chain"], g * DVE_LINKS)

                    def statistics():
                        eng.wait_ge(S["x_loaded"], g * 16 + 16)
                        for i in range(ST):
                            ch.add(eng.bn_stats(st6[:, i, :], x1[:, i, :]))
                        ch.settle()
                        ch.add(eng.memset(var1[:], 0.0))
                        for i in range(ST):
                            ch.add(eng.bn_aggr(mv[:, i, :], st6[:, i, :]))
                        ch.settle()
                        eng.tensor_scalar(var1[:], mv[:, :, 1], EPS_LN, None, ALU.add).then_inc(S["var_ready"], 1)
                        assert ch.n == DVE_LINKS, ch.n

                    def layer_norm():
                        eng.wait_ge(S["rstd_ready"], g + 1)
                        for i in range(ST):
                            eng.tensor_scalar(xl[:, i, :], x1[:, i, :], mv[:, i, 0:1], rstd[:, i:i + 1],
                                              ALU.subtract, ALU.mult).then_inc(S["xl_ready"], 1)

                    def mean_square():
                        eng.wait_ge(S["ssq_ready"], g * ST + ST)
                        eng.tensor_scalar(ms[:], ssq[:], 1.0 / DM, EPS_RMS_F, ALU.mult, ALU.add).then_inc(S["ms_ready"], 1)

                    def rms_norm():
                        eng.wait_ge(S["rrms_ready"], g + 1)
                        if not isinstance(g, int):
                            eng.wait_ge(S["tp_done"], g * ST)
                            eng.wait_ge(c.flat_stored, g * 16)
                        for i in range(ST):
                            eng.scalar_tensor_tensor(flat[:, i, :], xl[:, i, :], rrms[:, i:i + 1], norm_w[:],
                                                     ALU.mult, ALU.mult).then_inc(S["flat_ready"], 1)

                    return statistics, layer_norm, mean_square, rms_norm

                def work_steps(g):
                    def mult(i):
                        eng.wait_ge(S["silu_done"], g * ST + (i + 1))
                        eng.wait_ge(S["at_done"], g * ST + (i + 1))
                        eng.tensor_tensor(act[:, i % 2], gs[:, i % 2], bank[4 + 2 * (i % 2)][:], ALU.mult)\
                            .then_inc(S["act_ready"], 1)

                    def add(i):
                        eng.wait_ge(S["sd_done"], g * ST + (i + 1 + 2))
                        eng.wait_ge(S["base_ready"], g * ST + (i + 1))
                        b = c.base[:, bass.ds(g * ST + i, 1), :].rearrange("p a n -> p (a n)")
                        eng.tensor_tensor(b, b, bank[i % 2][:], ALU.add).then_inc(S["sd_added"], 1)

                    def logits(_):
                        eng.wait_ge(S["logits_done"], g + 1)
                        eng.tensor_scalar(c.logits[:, bass.ds(g * ST, ST), :],
                                          bank[2][:, 0:ST * E].rearrange("p (t e) -> p t e", t=ST),
                                          0.0, None, ALU.add).then_inc(S["logits_read"], 1)

                    return [lambda f=f, i=i: f(i) for f, i in (
                        (mult, 0), (mult, 1), (add, 0), (mult, 2), (add, 1), (mult, 3), (add, 2), (logits, 0), (add, 3))]

                interleaved(eng, norm_steps, work_steps, "wnwnwwnwnwwww")

            @block.gpsimd
            def _(eng):
                with eng.Fori(0, NG) as g:
                    for i in range(ST):
                        eng.wait_ge(S["xl_ready"], g * ST + (i + 1))
                        eng.tensor_tensor(c.base[:, bass.ds(g * ST + i, 1), :].rearrange("p a n -> p (a n)"),
                                          x1[:, i, :], xl[:, i, :], ALU.add).then_inc(S["base_ready"], 1)

            @block.tensor
            def _(eng):
                eng.sem_inc(S["at_done"], 2)
                eng.sem_inc(S["sd_done"], 2)
                eng.wait_ge(S["w_loaded"], 16 * len(loads))

                with eng.Fori(0, NG) as g:
                    def transposes(i):
                        eng.wait_ge(S["flat_ready"], g * ST + (i + 1))
                        if i < 2:
                            eng.wait_ge(S["sd_added"], g * ST + (i + 1))
                        eng.wait_ge(S["tp_evac"], g * ST + (i + 1))
                        for k in range(KC):
                            ins = eng.transpose(bank[i % 2][:, k * P:(k + 1) * P], flat[:, i, k * P:(k + 1) * P], c.ident[:])
                        ins.then_inc(S["tp_done"], 1)

                    def gate_up(i, between=lambda: None):
                        eng.wait_ge(S["tp_evac"], g * ST + (i + 1 + 2))
                        if i == 0:
                            eng.wait_ge(S["logits_read"], g + 1)
                        for k in range(KC):
                            ins = eng.matmul(bank[2][:, i * E:(i + 1) * E], flT[:, i, k, :], w_r[:, k, :],
                                             start=(k == 0), stop=(k == KC - 1))
                        if i == ST - 1:
                            ins.then_inc(S["logits_done"], 1)
                        eng.wait_ge(S["act_ready"], g * ST + (i + 1))
                        for w, o in ((w_g, 3), (w_u, 4)):
                            for k in range(KC):
                                ins = eng.matmul(bank[o + 2 * (i % 2)][:], flT[:, i, k, :], w[:, k, :],
                                                 start=(k == 0), stop=(k == KC - 1))
                            if w is w_g:
                                between()
                        ins.then_inc(S["gu_done"], 1)

                    def act_transposes(i):
                        eng.wait_ge(S["act_ready"], g * ST + (i + 1 + 2))
                        eng.wait_ge(S["at_evac"], g * ST + (i + 1))
                        for k in range(SH // P):
                            ins = eng.transpose(bank[7][:, k * P:(k + 1) * P], act[:, i % 2, k * P:(k + 1) * P], c.ident[:])
                        ins.then_inc(S["at_done"], 1)

                    def down(i):
                        eng.wait_ge(S["at_evac"], g * ST + (i + 1 + 1))
                        eng.wait_ge(S["sd_added"], g * ST + (i + 1))
                        for k in range(SH // P):
                            ins = eng.matmul(bank[i % 2][:], actT[:, i % 2, k, :], w_d[:, k, :],
                                             start=(k == 0), stop=(k == SH // P - 1))
                        ins.then_inc(S["sd_done"], 1)

                    transposes(0), transposes(1), gate_up(0), transposes(2), transposes(3)
                    gate_up(1, lambda: act_transposes(0))
                    eng.wait_ge(S["tp_evac"], g * ST + (ST + 2))
                    down(0), gate_up(2, lambda: act_transposes(1))
                    down(1), gate_up(3, lambda: act_transposes(2))
                    down(2), act_transposes(3), down(3)


def routing(nc, c, dram):
    ctx = ExitStack()
    with ctx:
        def sb(name, shape, dt=F32):
            return ctx.enter_context(nc.sbuf_tensor(name, shape, dt))

        rank_ps = ctx.enter_context(nc.psum_tensor("rank_ps", [P, TT * E], F32))
        count_ps = ctx.enter_context(nc.psum_tensor("count_ps", [P, 512], F32))
        list_ps = ctx.enter_context(nc.psum_tensor("list_ps", [P, 512], F32))
        mx, sm = sb("mx", [P, TT]), sb("sm", [P, TT])
        prob = sb("prob", [P, TT, E])
        top = sb("top", [P, TT, 8])
        top_i = sb("top_i", [P, TT, 8], U32)
        idx = sb("idx", [P, TT, TOPK])
        oh = sb("oh", [P, TOPK, TT, E])
        mask, cum = sb("mask", [P, TT, E]), sb("cum", [P, TT + 1, E])
        cnt, nt, end, zero = sb("cnt", [P, E]), sb("nt", [P, E]), sb("end", [P, E]), sb("zero", [P, E])
        off = sb("off", [P, E])
        NM = T // P
        cmp = sb("cmp", [P, E, NM])
        posn, hit = sb("posn", [P, TT, E]), sb("hit", [P, TT, E])
        lo_i, hi_i = sb("lo_i", [P, TT * TOPK], I32), sb("hi_i", [P, TT * TOPK], I32)
        dest_i = sb("dest_i", [P, TT * TOPK], I32)
        lo, hi = sb("lo", [P, TT * TOPK]), sb("hi", [P, TT * TOPK])
        iota_i, iota = sb("iota_i", [P, P], I32), sb("iota", [P, P])
        tok_i, tok = sb("tok_i", [P, TT], I32), sb("tok", [P, TT])
        thr_i, thr = sb("thr_i", [P, NM], I32), sb("thr", [P, NM])
        assert T <= 2048
        iota_h = sb("iota_h", [P, P], F16)
        oh_lo, oh_hi = sb("oh_lo", [P, 2, TOPK, P], F16), sb("oh_hi", [P, 2, TOPK, NT], F16)
        ecmp, etile = sb("ecmp", [P, E]), sb("etile", [P, 1])
        live = sb("live", [1, NT // PASS + 1])
        names = "iota_made chain max_ready exp_done mask_ready counted tiles_ready tiles_turned hot_ready placed".split()
        S = {n: ctx.enter_context(nc.semaphore("r_" + n)) for n in names}

        with nc.Block() as block:
            @block.gpsimd
            def _(eng):
                eng.iota(iota_i[:], pattern=[[1, P]], base=0, channel_multiplier=0).then_inc(S["iota_made"], 1)
                eng.iota(tok_i[:], pattern=[[P, TT]], base=0, channel_multiplier=1).then_inc(S["iota_made"], 1)
                eng.iota(thr_i[:], pattern=[[P, NM]], base=0, channel_multiplier=0).then_inc(S["iota_made"], 1)

            @block.scalar
            def _(eng):
                eng.wait_ge(S["max_ready"], 1)
                eng.activation(prob[:], prob[:], ACT.Exp).then_inc(S["exp_done"], 1)

            @block.vector
            def _(eng):
                ch = Chain(eng, S["chain"])
                row = lambda ap, n: ap.unsqueeze(2).to_broadcast([P, ap.shape[1], n])
                ch.add(eng.tensor_reduce(mx[:], c.logits[:], AX.X, ALU.max))
                ch.settle()
                eng.tensor_tensor(prob[:], c.logits[:], row(mx[:], E), ALU.subtract).then_inc(S["max_ready"], 1)
                eng.wait_ge(S["iota_made"], 3)
                for a, b in ((iota, iota_i), (iota_h, iota_i), (tok, tok_i), (thr, thr_i)):
                    ch.add(eng.tensor_copy(a[:], b[:]))
                ch.add(eng.memset(zero[:], 0.0))
                ch.add(eng.memset(cum[:, 0, :], 0.0))
                ch.add(eng.memset(c.dest[:, TT:, :], 0.0))
                ch.add(eng.memset(c.slot_token[:, NT:], 0.0))
                eng.wait_ge(S["exp_done"], 1)
                ch.add(eng.tensor_reduce(sm[:], prob[:], AX.X, ALU.add))
                ch.settle()
                ch.add(eng.reciprocal(sm[:], sm[:]))
                ch.settle()
                ch.add(eng.tensor_tensor(prob[:], prob[:], row(sm[:], E), ALU.mult))
                ch.settle()
                for t in range(TT):
                    ch.add(eng.max(top[:, t, :], prob[:, t, :]))
                ch.settle()
                for t in range(TT):
                    ch.add(eng.max_index(top_i[:, t, :], top[:, t, :], prob[:, t, :]))
                ch.add(eng.tensor_reduce(sm[:], top[:, :, 0:TOPK], AX.X, ALU.add))
                ch.settle()
                ch.add(eng.reciprocal(sm[:], sm[:]))
                ch.add(eng.tensor_copy(idx[:], top_i[:, :, 0:TOPK]))
                ch.settle()
                ch.add(eng.tensor_tensor(c.weight[:], top[:, :, 0:TOPK], row(sm[:], TOPK), ALU.mult))
                ex = iota[:, 0:E].unsqueeze(1).to_broadcast([P, TT, E])
                for k in range(TOPK):
                    ch.add(eng.tensor_tensor(oh[:, k], ex, row(idx[:, :, k], E), ALU.is_equal))
                ch.settle()
                ch.add(eng.tensor_tensor(mask[:], oh[:, 0], oh[:, 1], ALU.add))
                ch.add(eng.tensor_tensor(hit[:], oh[:, 2], oh[:, 3], ALU.add))
                ch.settle()
                ch.add(eng.tensor_tensor(mask[:], mask[:], hit[:], ALU.add))
                for t in range(TT):
                    ch.settle()
                    ch.add(eng.tensor_tensor(cum[:, t + 1, :], cum[:, t, :], mask[:, t, :], ALU.add))
                ch.settle()
                eng.memset(hit[:], 0.0).then_inc(S["mask_ready"], 1)
                eng.wait_ge(S["counted"], 1)
                ch.add(eng.tensor_copy(cnt[:], count_ps[:, 0:E]))
                ch.settle()
                ch.add(eng.tensor_tensor(cmp[:], row(cnt[:], NM), thr[:].unsqueeze(1).to_broadcast([P, E, NM]), ALU.is_gt))
                ch.settle()
                ch.add(eng.tensor_reduce(nt[:], cmp[:], AX.X, ALU.add))
                ch.settle()
                ch.add(eng.tensor_scalar(nt[:], nt[:], 1.0, None, ALU.max))
                ch.settle()
                ch.add(eng.tensor_tensor_scan(end[:], nt[:], zero[:], 0.0, ALU.add, ALU.add))
                ch.settle()
                ch.add(eng.tensor_tensor(off[:], end[:], nt[:], ALU.subtract))
                ch.add(eng.tensor_scalar(ecmp[:], end[:], tok[:, 0:1], None, ALU.is_le))
                ch.settle()
                ch.add(eng.tensor_reduce(etile[:], ecmp[:], AX.X, ALU.add))
                ch.settle()
                eng.tensor_scalar(etile[:], etile[:], float(E - 1), None, ALU.min).then_inc(S["tiles_ready"], 1)
                ch.add(eng.tensor_scalar(off[:], off[:], float(P), None, ALU.mult))
                ch.settle()
                ch.add(eng.tensor_tensor(posn[:], rank_ps[:].rearrange("p (t e) -> p t e", t=TT),
                                         off[:].unsqueeze(1).to_broadcast([P, TT, E]), ALU.add))
                for k in range(TOPK):
                    ch.settle()
                    ch.add(eng.tensor_tensor(hit[:], oh[:, k], posn[:], ALU.mult))
                    ch.settle()
                    ch.add(eng.tensor_reduce(c.dest[:, 0:TT, k], hit[:], AX.X, ALU.add))
                ch.settle()
                flat_dest = c.dest[:, 0:TT, :].rearrange("p t k -> p (t k)")
                ch.add(eng.tensor_copy(dest_i[:], flat_dest))
                ch.settle()
                ch.add(eng.tensor_scalar(lo_i[:], dest_i[:], P - 1, None, ALU.bitwise_and))
                ch.add(eng.tensor_scalar(hi_i[:], dest_i[:], P.bit_length() - 1, None, ALU.arith_shift_right))
                ch.settle()
                ch.add(eng.tensor_copy(lo[:], lo_i[:]))
                ch.add(eng.tensor_copy(hi[:], hi_i[:]))
                ch.settle()
                eng.wait_ge(S["tiles_turned"], 1)
                ch.add(eng.tensor_scalar(c.tile_need[:], count_ps[0:1, E:E + NT], 1.0, None, ALU.add))
                ch.add(eng.tensor_copy(c.tile_ring[:], count_ps[0:1, E:E + NT]))
                ch.add(eng.memset(live[:, 0:1], 1.0))
                ch.add(eng.tensor_scalar(live[:, 1:], iota[0:1, 0:NT // PASS], float(PASS), end[0:1, E - 1:E],
                                         ALU.mult, ALU.is_lt))
                ch.add(eng.tensor_scalar(c.expert_end[:], end[0:1, :], 1.0, None, ALU.add))
                ch.settle()
                ch.add(eng.tensor_copy(c.pass_live[:], live[:]))
                ch.add(eng.tensor_scalar(c.tile_ring[:], c.tile_ring[:], RING - 1, None, ALU.bitwise_and))
                eng.sem_inc(S["placed"], 2)
                with eng.Fori(0, TT // 2) as r:
                    for u in (0, 1):
                        t = r * 2 + u
                        eng.wait_ge(S["placed"], t + 1)
                        for k in range(TOPK):
                            at = bass.ds(t * TOPK + k, 1)
                            eng.tensor_scalar(oh_lo[:, u, k], iota_h[:], lo[:, at], None, ALU.is_equal)\
                                .then_inc(S["hot_ready"], 1)
                            eng.tensor_scalar(oh_hi[:, u, k], iota_h[:, 0:NT], hi[:, at], tok[:, bass.ds(t, 1)],
                                              ALU.is_equal, ALU.mult).then_inc(S["hot_ready"], 1)
                eng.wait_ge(S["placed"], TT + 2)
                ch.add(eng.tensor_copy(c.slot_token[:, 0:NT], list_ps[:, 0:NT]))
                ch.settle()

            @block.tensor
            def _(eng):
                eng.wait_ge(S["mask_ready"], 1)
                eng.matmul(rank_ps[:], c.tri[:], mask[:].rearrange("p t e -> p (t e)"), start=True, stop=False)
                eng.matmul(rank_ps[:], c.ones[:], cum[:, 0:TT, :].rearrange("p t e -> p (t e)"), start=False, stop=True)
                eng.matmul(count_ps[:, 0:E], c.ones[:], cum[:, TT, :], start=True, stop=True).then_inc(S["counted"], 1)

                eng.wait_ge(S["tiles_ready"], 1)
                eng.matmul(count_ps[0:1, E:E + NT], etile[:], c.ident[:, 0:NT], start=True, stop=True)\
                    .then_inc(S["tiles_turned"], 1)

                def place(t, u, first=False, last=False):
                    eng.wait_ge(S["hot_ready"], t * (2 * TOPK) + 2 * TOPK)
                    for k in range(TOPK):
                        ins = eng.matmul(list_ps[:, 0:NT], oh_lo[:, u, k], oh_hi[:, u, k], skip_group_check=True,
                                         start=(first and k == 0), stop=(last and k == TOPK - 1))
                    ins.then_inc(S["placed"], 1)

                place(0, 0, first=True)
                place(1, 1)
                with eng.Fori(1, TT // 2 - 1) as r:
                    for u in (0, 1):
                        place(r * 2 + u, u)
                place(TT - 2, 0)
                place(TT - 1, 1, last=True)


def experts(nc, c, dram):
    ctx = ExitStack()
    with ctx:
        def sb(name, shape, dt=F32):
            return ctx.enter_context(nc.sbuf_tensor(name, shape, dt))

        U = PASS
        xT_ps = [ctx.enter_context(nc.psum_tensor(f"xT_ps{i}", [P, 512], F32)) for i in range(2)]
        h_ps = [ctx.enter_context(nc.psum_tensor(f"h_ps{i}", [P, 512], F32)) for i in range(2)]
        aT_ps = [ctx.enter_context(nc.psum_tensor(f"aT_ps{i}", [P, 512], F32)) for i in range(2)]
        y_ps = [ctx.enter_context(nc.psum_tensor(f"y_ps{i}", [P, 512], F32)) for i in range(2)]
        which = sb("which", [P, U], I32)
        xg = sb("xg", [P, U, DM])
        held = sb("held", [P, 1])
        xT = sb("xT", [P, 2, KC, P])
        gs = sb("gs", [P, 2, FI])
        act = sb("act", [P, 2, FI])
        aT = sb("aT", [P, 2, FC, P])
        y = sb("y", [P, U, DM])
        names = ("which_ready xT_done xT_ready h_done silu_done act_ready aT_done aT_ready y_done y_ready "
                 "expert_ready held").split()
        S = {n: ctx.enter_context(nc.semaphore("e_" + n)) for n in names}
        gathered = [ctx.enter_context(nc.semaphore(f"e_gathered{u}")) for u in range(U)]
        stored = [ctx.enter_context(nc.semaphore(f"e_stored{u}")) for u in range(U)]

        def live(eng, column):
            return eng.value_load(c.pass_live[0:1, bass.ds(column, 1)], min_val=0, max_val=1)

        def tiles(eng, body):
            with eng.Fori(0, NT // U) as r:
                with eng.If(live(eng, r + 1) > 0):
                    for p in range(0, U, 2):
                        body(r, p)

        with nc.Block() as block:
            @block.sync
            def _(eng):
                for e in range(RING - 1):
                    eng.wait_ge(c.w_landed[e], 32)
                    eng.sem_inc(S["expert_ready"], 1)
                with eng.Fori(0, E // RING - 1) as r:
                    for u in range(RING):
                        last = eng.value_load(c.expert_end[0:1, bass.ds(r * RING + u, 1)], min_val=1, max_val=NT + 1)
                        eng.wait_ge(S["y_done"], last)
                        ds = bass.ds(r * RING + (RING + u), 1)
                        eng.dma_start(c.w1r[:, u], dram.w1[ds].rearrange("a p k n -> (a p) k n")).then_inc(c.w_landed[u], 16)
                        eng.dma_start(c.w2r[:, u], dram.w2[ds].rearrange("a p k n -> (a p) k n")).then_inc(c.w_landed[u], 16)
                        prev = (u - 1) % RING
                        eng.wait_ge(c.w_landed[prev], r * 32 + (32 if u == 0 else 64))
                        eng.sem_inc(S["expert_ready"], 1)
                eng.wait_ge(c.w_landed[RING - 1], E // RING * 32)
                eng.sem_inc(S["expert_ready"], 1)

            @block.gpsimd
            def _(eng):
                eng.sem_inc(S["held"], 1)
                def gather(r, u):
                        eng.wait_ge(S["xT_done"], r * U + (u + 1))
                        eng.wait_ge(S["which_ready"], r * U + (u + 1))
                        eng.wait_ge(S["held"], r * U + (u + 1))
                        eng.tensor_tensor(held[:], c.ones[:, 0:1], c.ones[:, 0:1], ALU.mult).then_inc(S["held"], 1)
                        eng.indirect_dma_start(out=xg[:, u, :], out_offset=None, in_=dram.flat,
                                               in_offset=bass.IndirectOffsetOnAxis(ap=which[:, u:u + 1], axis=0))\
                            .then_inc(gathered[u], 16)

                with eng.Fori(0, NT // U) as r:
                    with eng.If(live(eng, r) > 0):
                        for u in (0, 1):
                            gather(r, u)
                    with eng.If(live(eng, r + 1) > 0):
                        for u in (2, 3):
                            gather(r, u)
                with eng.If(live(eng, NT // U) > 0):
                    for u in (0, 1):
                        gather(NT // U, u)

            @block.scalar
            def _(eng):
                for u in range(U):
                    eng.sem_inc(stored[u], 16)
                eng.sem_inc(S["aT_ready"], 2)

                def pair(r, p):
                    for i in (0, 1):
                        j = r * U + (p + i)
                        eng.wait_ge(S["h_done"], j + 1)
                        eng.wait_ge(S["act_ready"], j + 1)
                        eng.activation(gs[:, i], h_ps[i][:, 0:FI], ACT.Silu).then_inc(S["silu_done"], 1)
                    for i in (0, 1):
                        j = r * U + (p + i)
                        eng.wait_ge(S["aT_done"], j + (1 + 2))
                        eng.activation(aT[:, i], aT_ps[i][:, 0:FI].rearrange("p (k t) -> p k t", k=FC), ACT.Copy)\
                            .then_inc(S["aT_ready"], 1)
                    for i in (0, 1):
                        j = r * U + (p + i)
                        eng.wait_ge(S["y_ready"], j + (1 + 2))
                        eng.dma_start(dram.ys[bass.ds(j, 1)].rearrange("a p n -> (a p) n"), y[:, p + i, :])\
                            .then_inc(stored[p + i], 16)

                with eng.Fori(0, NT // U) as r:
                    alive = live(eng, r + 1)
                    with eng.If(alive > 0):
                        for p in range(0, U, 2):
                            pair(r, p)
                    with eng.Else():
                        for u in range(U):
                            eng.sem_inc(stored[u], 16)
                for u in range(U):
                    eng.wait_ge(stored[u], NT // U * 16 + 16)

            @block.vector
            def _(eng):
                eng.sem_inc(S["act_ready"], 2)
                eng.sem_inc(S["y_ready"], 2)
                eng.sem_inc(S["xT_ready"], 2)
                for u in range(U):
                    eng.tensor_copy(which[:, u:u + 1], c.slot_token[:, u:u + 1]).then_inc(S["which_ready"], 1)

                def rows_out(j, i):
                    eng.wait_ge(S["xT_done"], j + (1 + U))
                    eng.tensor_scalar(xT[:, i], xT_ps[i][:].rearrange("p (k t) -> p k t", k=KC), 0.0, None, ALU.add)\
                        .then_inc(S["xT_ready"], 1)

                def pair(r, p):
                    for i in (0, 1):
                        j = r * U + (p + i)
                        eng.wait_ge(S["silu_done"], j + 1)
                        eng.wait_ge(S["aT_done"], j + 1)
                        eng.tensor_tensor(act[:, i], gs[:, i], h_ps[i][:, FI:2 * FI], ALU.mult).then_inc(S["act_ready"], 1)
                    for i in (0, 1):
                        rows_out(r * U + (p + i + 2), i)
                    for i in (0, 1):
                        eng.wait_ge(gathered[p + i], r * 16 + 16)
                        eng.tensor_scalar(which[:, p + i:p + i + 1], c.slot_token[:, bass.ds(r * U + (p + i + U), 1)], 0.0, None,
                                          ALU.add).then_inc(S["which_ready"], 1)
                    for i in (0, 1):
                        j = r * U + (p + i)
                        eng.wait_ge(S["y_done"], j + 2)
                        eng.wait_ge(stored[p + i], r * 16 + 16)
                        eng.tensor_scalar(y[:, p + i, :], y_ps[i][:], 0.0, None, ALU.add).then_inc(S["y_ready"], 1)

                for i in (0, 1):
                    rows_out(i, i)
                tiles(eng, pair)

            @block.tensor
            def _(eng):
                eng.sem_inc(S["xT_done"], U)
                eng.sem_inc(S["aT_done"], 2)
                eng.sem_inc(S["y_done"], 1)

                def rows_in(j, p, i, pass_):
                    eng.wait_ge(gathered[p + i], pass_ * 16 + 16)
                    eng.wait_ge(S["xT_ready"], j + 1)
                    for k in range(KC):
                        ins = eng.transpose(xT_ps[i][:, k * P:(k + 1) * P], xg[:, p + i, k * P:(k + 1) * P], c.ident[:])
                    ins.then_inc(S["xT_done"], 1)

                def pair(r, p):
                    ring = []
                    for i in (0, 1):
                        j = r * U + (p + i)
                        ring.append(eng.value_load(c.tile_ring[0:1, bass.ds(j, 1)], min_val=0, max_val=RING - 1))
                        need = eng.value_load(c.tile_need[0:1, bass.ds(j, 1)], min_val=1, max_val=E)
                        eng.wait_ge(S["expert_ready"], need)
                        eng.wait_ge(S["xT_ready"], j + (1 + 2))
                        eng.wait_ge(S["act_ready"], j + 1)
                        for k in range(KC):
                            ins = eng.matmul(h_ps[i][:], xT[:, i, k, :], c.w1r[:, bass.ds(ring[i], 1), k, :].rearrange("p a n -> p (a n)"),
                                             start=(k == 0), stop=(k == KC - 1))
                        ins.then_inc(S["h_done"], 1)
                    for i in (0, 1):
                        rows_in(r * U + (p + i + 2), (p + 2) % U, i, r + (p + 2) // U)
                    for i in (0, 1):
                        j = r * U + (p + i)
                        eng.wait_ge(S["act_ready"], j + (1 + 2))
                        eng.wait_ge(S["aT_ready"], j + 1)
                        for k in range(FC):
                            ins = eng.transpose(aT_ps[i][:, k * P:(k + 1) * P], act[:, i, k * P:(k + 1) * P], c.ident[:])
                        ins.then_inc(S["aT_done"], 1)
                    for i in (0, 1):
                        j = r * U + (p + i)
                        eng.wait_ge(S["aT_ready"], j + (1 + 2))
                        eng.wait_ge(S["y_ready"], j + 1)
                        for k in range(FC):
                            ins = eng.matmul(y_ps[i][:], aT[:, i, k, :], c.w2r[:, bass.ds(ring[i], 1), k, :].rearrange("p a n -> p (a n)"),
                                             start=(k == 0), stop=(k == FC - 1))
                        ins.then_inc(S["y_done"], 1)

                for i in (0, 1):
                    rows_in(i, 0, i, 0)
                tiles(eng, pair)


def combine(nc, c, dram):
    ctx = ExitStack()
    with ctx:
        def sb(name, shape, dt=F32):
            return ctx.enter_context(nc.sbuf_tensor(name, shape, dt))

        U = COMBINED
        where = sb("where", [P, U, TOPK], I32)
        rows = sb("rows", [P, U, TOPK, DM])
        held = sb("c_held", [P, 1])
        names = "where_ready added summed held".split()
        S = {n: ctx.enter_context(nc.semaphore("c_" + n)) for n in names}
        gathered = [ctx.enter_context(nc.semaphore(f"c_gathered{u}")) for u in range(U)]
        stored = ctx.enter_context(nc.semaphore("c_stored"))

        with nc.Block() as block:
            @block.gpsimd
            def _(eng):
                eng.sem_inc(S["held"], 1)
                with eng.Fori(0, TT // U) as r:
                    for u in range(U):
                        t = r * U + u
                        eng.wait_ge(S["summed"], t + 1)
                        eng.wait_ge(S["where_ready"], t + 1)
                        eng.wait_ge(S["held"], t + 1)
                        eng.tensor_tensor(held[:], c.ones[:, 0:1], c.ones[:, 0:1], ALU.mult).then_inc(S["held"], 1)
                        for k in range(TOPK):
                            eng.indirect_dma_start(out=rows[:, u, k, :], out_offset=None, in_=dram.ys_rows,
                                                   in_offset=bass.IndirectOffsetOnAxis(ap=where[:, u, k:k + 1], axis=0))\
                                .then_inc(gathered[u], 16)

            @block.vector
            def _(eng):
                eng.sem_inc(S["summed"], U)
                for u in range(U):
                    eng.tensor_copy(where[:, u, :], c.dest[:, u, :]).then_inc(S["where_ready"], 1)
                with eng.Fori(0, TT // U) as r:
                    for u in range(U):
                        t = r * U + u
                        b = c.base[:, bass.ds(t, 1), :].rearrange("p a n -> p (a n)")
                        eng.wait_ge(gathered[u], r * (16 * TOPK) + 16 * TOPK)
                        eng.tensor_scalar(where[:, u, :], c.dest[:, bass.ds(t + U, 1), :].rearrange("p a k -> p (a k)"), 0.0,
                                          None, ALU.add).then_inc(S["where_ready"], 1)
                        for k in range(TOPK):
                            if k:
                                eng.wait_ge(S["added"], t * (TOPK - 1) + k)
                            w = c.weight[:, bass.ds(t, 1), k:k + 1].rearrange("p a k -> p (a k)")
                            eng.scalar_tensor_tensor(b, rows[:, u, k, :], w, b, ALU.mult, ALU.add)\
                                .then_inc(S["added" if k < TOPK - 1 else "summed"], 1)

            @block.sync
            def _(eng):
                with eng.Fori(0, TT) as t:
                    eng.wait_ge(S["summed"], t + (1 + U))
                    eng.dma_start(dram.out[bass.ds(t, 1)].rearrange("a p n -> (a p) n"),
                                  c.base[:, bass.ds(t, 1), :].rearrange("p a n -> p (a n)")).then_inc(stored, 16)
                eng.wait_ge(stored, 16 * TT)


def build(nc, dram):
    class Shared:
        pass

    c = Shared()
    with ExitStack() as ctx:
        def sb(name, shape, dt=F32):
            return ctx.enter_context(nc.sbuf_tensor(name, shape, dt))

        constants(nc, c, ctx, dram)
        mamba(nc, c, dram)
        c.base = sb("base", [P, TT, DM])
        c.logits = sb("logits", [P, TT, E])
        c.weight = sb("weight", [P, TT, TOPK])
        c.dest = sb("dest", [P, TT + COMBINED, TOPK])
        c.slot_token = sb("slot_token", [P, NT + RING])
        c.tile_ring, c.tile_need = sb("tile_ring", [1, NT], I32), sb("tile_need", [1, NT], I32)
        c.expert_end = sb("expert_end", [1, E], I32)
        c.pass_live = sb("pass_live", [1, NT // PASS + 1], I32)
        c.w1r, c.w2r = sb("w1_ring", [P, RING, KC, 2 * FI]), sb("w2_ring", [P, RING, FC, DM])
        c.w_landed = [ctx.enter_context(nc.semaphore(f"w_landed{u}")) for u in range(RING)]
        c.flat_stored = ctx.enter_context(nc.semaphore("flat_stored"))
        tokens(nc, c, dram)
        routing(nc, c, dram)
        experts(nc, c, dram)
        combine(nc, c, dram)


class Dram:
    pass


def tensors(nc, arrays):
    def given(name):
        a = arrays[name]
        return nc.dram_tensor("in_" + name, a.shape, mybir.dt.from_np(a.dtype), kind="ExternalInput").ap()

    d = Dram()
    d.x, d.w_norm = given("x"), given("w_norm")
    d.w_in_x, d.w_in_res = given("w_in_x"), given("w_in_res")
    d.conv_w, d.conv_b = given("conv_w"), given("conv_b")
    d.b_dt, d.d_skip, d.a_log = given("b_dt"), given("d_skip"), given("a_log")
    d.w_xp, d.w_dt, d.w_out = given("w_xp"), given("w_dt"), given("w_out")
    d.norm_w, d.router_w = given("norm_w"), given("router_w")
    d.sg, d.su, d.sd = given("sg"), given("su"), given("sd")
    d.w1, d.w2 = given("w1"), given("w2")
    d.bcd = nc.dram_tensor("bcd", (NB * HALVES, 2 * NS, SEG), F32, kind="Internal").ap()
    d.out = nc.dram_tensor("out", (TT, P, DM), F32, kind="ExternalOutput").ap()
    d.x1 = nc.dram_tensor("x1", (TT, P, DM), F32, kind="Internal").ap()
    d.flat = nc.dram_tensor("flat", (T, DM), F32, kind="Internal").ap()
    d.flat_seg = d.flat.rearrange("(s t p) n -> s p t n", t=ST, p=P)
    d.ys = nc.dram_tensor("ys", (NT, P, DM), F32, kind="Internal").ap()
    d.ys_rows = d.ys.rearrange("j p n -> (j p) n")
    d.x_seg = d.x.rearrange("(s t) p n -> s p t n", t=ST)
    d.x1_seg = d.x1.rearrange("(s t) p n -> s p t n", t=ST)
    return d


def kernel(**inputs):
    import concourse.bacc as bacc
    from concourse.bass_utils import run_bass_kernel_spmd as run

    g = {k: np.asarray(v) for k, v in inputs.items()}
    a = lambda n: g["L0_attn_" + n]
    cont = np.ascontiguousarray
    col = lambda v, *rest: cont(np.moveaxis(v.reshape(-1, P, *rest), 0, 1))
    w_in = a("W_in").reshape(KC, P, 2, DC, P)
    arrays = {
        "x": cont(a("x").reshape(TT, P, DM)),
        "w_norm": cont(a("w_norm").reshape(1, DM)),
        "w_in_x": cont(w_in[:, :, 0].reshape(KC, P, DI).transpose(1, 0, 2)),
        "w_in_res": cont(w_in[:, :, 1].transpose(2, 1, 0, 3)),
        "conv_w": cont(a("conv_w").reshape(KW, DC, P).transpose(2, 1, 0)),
        "conv_b": col(a("conv_b")), "b_dt": col(a("b_dt")), "d_skip": col(a("D")),
        "a_log": cont(a("A_log").reshape(DC, P, NS).transpose(1, 0, 2).reshape(P, DC * NS)),
        "w_xp": col(a("W_xp"), DR + 2 * NS),
        "w_dt": cont(a("W_dt").reshape(DR, DC, P).transpose(1, 0, 2)),
        "w_out": col(a("W_out"), DM),
        "norm_w": cont(g["L0_ffn_norm_w"].reshape(1, DM)),
        "router_w": col(g["L0_ffn_router_w"].T, E),
        "sg": col(g["L0_ffn_sg"], SH), "su": col(g["L0_ffn_su"], SH), "sd": col(g["L0_ffn_sd"], DM),
        "w1": cont(g["L0_ffn_w1"].reshape(E, KC, P, 2 * FI).transpose(0, 2, 1, 3)),
        "w2": cont(g["L0_ffn_w2"].reshape(E, FC, P, DM).transpose(0, 2, 1, 3)),
    }
    nc = bacc.Bacc("TRN2", target_bir_lowering=False, num_devices=1)
    dram = tensors(nc, arrays)
    build(nc, dram)
    r = run(nc, [{"in_" + n: v for n, v in arrays.items()}], core_ids=[0])
    return r.results[0]["out"].reshape(NB, LEN, DM)
```
